# Optimizing a Trainium2 kernel written in Bass

```python
import numpy as np
import jax
import jax.numpy as jnp

def _softmax(x, axis=-1):
    return jax.nn.softmax(x, axis=axis)

def _gelu(x):
    return jax.nn.gelu(x, approximate=True)

def _silu(x):
    return jax.nn.silu(x)

def _sigmoid(x):
    return jax.nn.sigmoid(x)

def _layernorm(x, axis=-1, eps=1e-05):
    m = jnp.mean(x, axis=axis, keepdims=True)
    v = jnp.var(x, axis=axis, keepdims=True)
    return (x - m) / jnp.sqrt(v + eps)

def _scatter_add(tgt, idx, src, axis=0):
    return tgt.at[idx].add(src)

def _segment_sum(src, seg, n):
    return jax.ops.segment_sum(src, seg, n)
kernel_name = 'mk_adaln_d2_jaxref_r8_0104d7'

def setup_inputs(seed: int=0):
    np.random.seed(seed)
    _w = jnp.asarray

    def _L0_attn_setup():
        import jax, jax.numpy as jnp
        import numpy as np
        B, N, C = (2, 256, 128)
        H = 16
        HD = C // H
        KA_IN = 2 * HD
        KA_OUT = HD
        T = 4
        KA_HID = KA_IN // 2
        KA_O = KA_OUT // T
        TEMPERATURE = 0.72
        SCALE = HD ** (-0.5)
        LN_EPS = 1e-05
        key = jax.random.key(seed)
        ks = jax.random.split(key, 20)

        def w(k, shape, fan_in):
            return jax.random.normal(k, shape, jnp.float32) / np.sqrt(fan_in)
        return {'x': jax.random.normal(ks[0], (B, N, C), jnp.float32), 'Wqkv': w(ks[1], (C, 3 * C), C), 'Wproj': w(ks[2], (C, C), C), 'bproj': jnp.zeros((C,), jnp.float32), 'alpha': jnp.ones((H,), jnp.float32), 'beta': jnp.ones((H,), jnp.float32), 'gamma': jnp.ones((H,), jnp.float32), 'A': w(ks[3], (T, KA_IN, KA_IN), KA_IN), 'Wphi1': w(ks[4], (T, KA_IN, KA_HID), KA_IN), 'bphi1': jnp.zeros((T, KA_HID), jnp.float32), 'Wphi2': w(ks[5], (T, KA_HID, KA_O), KA_HID), 'bphi2': jnp.zeros((T, KA_O), jnp.float32), 'Wpsi1': w(ks[6], (T, KA_IN, KA_IN), KA_IN), 'bpsi1': jnp.zeros((T, KA_IN), jnp.float32), 'ln_g': jnp.ones((T, KA_IN), jnp.float32), 'ln_b': jnp.zeros((T, KA_IN), jnp.float32), 'Wpsi2': w(ks[7], (T, KA_IN, KA_O), KA_IN), 'bpsi2': jnp.zeros((T, KA_O), jnp.float32), 'mixing': jnp.full((T,), 1.0 / T, jnp.float32), 'temp_scale': jnp.asarray(TEMPERATURE, jnp.float32)}
    _L0_attn_in = _L0_attn_setup()

    def _L0_ffn_setup():
        import jax, jax.numpy as jnp
        import numpy as np
        TOP_K = 2
        key = jax.random.key(seed)
        k1, k2, k3, k4, k5 = jax.random.split(key, 5)
        B, S, D, F, E = (2, 128, 128, 256, 8)
        return {'x': jax.random.normal(k1, (B, S, D), dtype=jnp.float32), 'router_kernel_DE': jax.random.normal(k2, (D, E), dtype=jnp.float32) * 0.02, 'kernel_gating_EDF': jax.random.normal(k3, (E, D, F), dtype=jnp.float32) * 0.02, 'kernel_up_EDF': jax.random.normal(k4, (E, D, F), dtype=jnp.float32) * 0.02, 'kernel_down_EFD': jax.random.normal(k5, (E, F, D), dtype=jnp.float32) * 0.02}
    _L0_ffn_in = _L0_ffn_setup()
    _L0_c = _w((lambda *s: np.random.randn(*s).astype(np.float32) * 0.05)(8, 128))
    _L0_wmod = _w((lambda *s: np.random.randn(*s).astype(np.float32) * 0.05)(128, 6 * 128) * 128 ** (-0.5))

    def _L1_attn_setup():
        import jax, jax.numpy as jnp
        import numpy as np
        NUM_HEADS = 16

        def _stablemax3_s(x):
            pos = 1.0 + x * (1.0 + 0.5 * x * (1.0 + x / 3.0))
            neg = 1.0 / (1.0 - x * (1.0 - 0.5 * x * (1.0 - x / 3.0)))
            return jnp.where(x >= 0, pos, neg)

        def stablemax3(logits, axis=-1):
            logits = logits - jnp.max(logits, axis=axis, keepdims=True)
            s = _stablemax3_s(logits)
            return s / jnp.sum(s, axis=axis, keepdims=True)
        key = jax.random.key(seed)
        k1, k2, k3 = jax.random.split(key, 3)
        B, S, D = (2, 256, 128)
        x = jax.random.normal(k1, (B, S, D), dtype=jnp.float32)
        w_qkv = jax.random.normal(k2, (3 * D, D), dtype=jnp.float32) * 0.02
        w_out = jax.random.normal(k3, (D, D), dtype=jnp.float32) * 0.02
        b_out = jnp.zeros((D,), dtype=jnp.float32)
        return {'x': x, 'w_qkv': w_qkv, 'w_out': w_out, 'b_out': b_out}
    _L1_attn_in = _L1_attn_setup()

    def _L1_ffn_setup():
        import jax, jax.numpy as jnp
        import numpy as np
        TOPK = 4
        key = jax.random.key(seed)
        ks = jax.random.split(key, 9)
        B, T, D = (4, 256, 128)
        E, H = (32, 128)
        HS = H * TOPK
        s = lambda k, shape, fan: jax.random.normal(k, shape, dtype=jnp.float32) / np.sqrt(fan)
        return {'x': jax.random.normal(ks[0], (B, T, D), dtype=jnp.float32), 'router_w': s(ks[1], (E, D), D), 'router_bias': jnp.zeros((E,), dtype=jnp.float32), 'gate_w': s(ks[2], (E, H, D), D), 'up_w': s(ks[3], (E, H, D), D), 'down_w': s(ks[4], (E, D, H), H), 'sgate_w': s(ks[5], (HS, D), D), 'sup_w': s(ks[6], (HS, D), D), 'sdown_w': s(ks[7], (D, HS), HS)}
    _L1_ffn_in = _L1_ffn_setup()
    _L1_c = _w((lambda *s: np.random.randn(*s).astype(np.float32) * 0.05)(8, 128))
    _L1_wmod = _w((lambda *s: np.random.randn(*s).astype(np.float32) * 0.05)(128, 6 * 128) * 128 ** (-0.5))
    _d = {'L0_attn_x': _L0_attn_in['x'], 'L0_attn_Wqkv': _L0_attn_in['Wqkv'], 'L0_attn_Wproj': _L0_attn_in['Wproj'], 'L0_attn_bproj': _L0_attn_in['bproj'], 'L0_attn_alpha': _L0_attn_in['alpha'], 'L0_attn_beta': _L0_attn_in['beta'], 'L0_attn_gamma': _L0_attn_in['gamma'], 'L0_attn_A': _L0_attn_in['A'], 'L0_attn_Wphi1': _L0_attn_in['Wphi1'], 'L0_attn_bphi1': _L0_attn_in['bphi1'], 'L0_attn_Wphi2': _L0_attn_in['Wphi2'], 'L0_attn_bphi2': _L0_attn_in['bphi2'], 'L0_attn_Wpsi1': _L0_attn_in['Wpsi1'], 'L0_attn_bpsi1': _L0_attn_in['bpsi1'], 'L0_attn_ln_g': _L0_attn_in['ln_g'], 'L0_attn_ln_b': _L0_attn_in['ln_b'], 'L0_attn_Wpsi2': _L0_attn_in['Wpsi2'], 'L0_attn_bpsi2': _L0_attn_in['bpsi2'], 'L0_attn_mixing': _L0_attn_in['mixing'], 'L0_attn_temp_scale': _L0_attn_in['temp_scale'], 'L0_ffn_router_kernel_DE': _L0_ffn_in['router_kernel_DE'], 'L0_ffn_kernel_gating_EDF': _L0_ffn_in['kernel_gating_EDF'], 'L0_ffn_kernel_up_EDF': _L0_ffn_in['kernel_up_EDF'], 'L0_ffn_kernel_down_EFD': _L0_ffn_in['kernel_down_EFD'], 'L0_c': _L0_c, 'L0_wmod': _L0_wmod, 'L1_attn_w_qkv': _L1_attn_in['w_qkv'], 'L1_attn_w_out': _L1_attn_in['w_out'], 'L1_attn_b_out': _L1_attn_in['b_out'], 'L1_ffn_router_w': _L1_ffn_in['router_w'], 'L1_ffn_router_bias': _L1_ffn_in['router_bias'], 'L1_ffn_gate_w': _L1_ffn_in['gate_w'], 'L1_ffn_up_w': _L1_ffn_in['up_w'], 'L1_ffn_down_w': _L1_ffn_in['down_w'], 'L1_ffn_sgate_w': _L1_ffn_in['sgate_w'], 'L1_ffn_sup_w': _L1_ffn_in['sup_w'], 'L1_ffn_sdown_w': _L1_ffn_in['sdown_w'], 'L1_c': _L1_c, 'L1_wmod': _L1_wmod}
    _x0 = _d['L0_attn_x']
    _d['L0_attn_x'] = jax.random.normal(jax.random.fold_in(jax.random.key(seed), 1), (8, 512, 128), dtype=_x0.dtype)
    del _x0
    return _d

def reference(L0_attn_x, L0_attn_Wqkv, L0_attn_Wproj, L0_attn_bproj, L0_attn_alpha, L0_attn_beta, L0_attn_gamma, L0_attn_A, L0_attn_Wphi1, L0_attn_bphi1, L0_attn_Wphi2, L0_attn_bphi2, L0_attn_Wpsi1, L0_attn_bpsi1, L0_attn_ln_g, L0_attn_ln_b, L0_attn_Wpsi2, L0_attn_bpsi2, L0_attn_mixing, L0_attn_temp_scale, L0_ffn_router_kernel_DE, L0_ffn_kernel_gating_EDF, L0_ffn_kernel_up_EDF, L0_ffn_kernel_down_EFD, L0_c, L0_wmod, L1_attn_w_qkv, L1_attn_w_out, L1_attn_b_out, L1_ffn_router_w, L1_ffn_router_bias, L1_ffn_gate_w, L1_ffn_up_w, L1_ffn_down_w, L1_ffn_sgate_w, L1_ffn_sup_w, L1_ffn_sdown_w, L1_c, L1_wmod):

    def _L0_attn_ref(x, Wqkv, Wproj, bproj, alpha, beta, gamma, A, Wphi1, bphi1, Wphi2, bphi2, Wpsi1, bpsi1, ln_g, ln_b, Wpsi2, bpsi2, mixing, temp_scale):
        import jax, jax.numpy as jnp
        import numpy as np
        B, N, C = (2, 256, 128)
        H = 16
        HD = C // H
        KA_IN = 2 * HD
        KA_OUT = HD
        T = 4
        KA_HID = KA_IN // 2
        KA_O = KA_OUT // T
        TEMPERATURE = 0.72
        SCALE = HD ** (-0.5)
        LN_EPS = 1e-05
        Bx, Nx, Cx = x.shape
        qkv = (x @ Wqkv).reshape(Bx, Nx, 3, H, HD).transpose(2, 0, 3, 1, 4)
        q, k, v = (qkv[0], qkv[1], qkv[2])
        attn = jnp.einsum('bhnd,bhmd->bhnm', q, k) * (SCALE / TEMPERATURE)
        attn = attn * alpha[None, :, None, None] + beta[None, :, None, None]
        attn = jax.nn.softmax(attn, axis=-1) * gamma[None, :, None, None]
        qk = jnp.concatenate([q.mean(-2), k.mean(-2)], -1).reshape(Bx * H, KA_IN)
        Ax = jnp.einsum('md,tde->tme', qk, A)
        phi = jax.nn.silu(jnp.einsum('md,tdh->tmh', qk, Wphi1) + bphi1[:, None, :])
        phi = jnp.einsum('tmh,tho->tmo', phi, Wphi2) + bphi2[:, None, :]
        psi = jnp.einsum('tme,teg->tmg', Ax, Wpsi1) + bpsi1[:, None, :]
        mu = psi.mean(-1, keepdims=True)
        var = ((psi - mu) ** 2).mean(-1, keepdims=True)
        psi = (psi - mu) / jnp.sqrt(var + LN_EPS) * ln_g[:, None, :] + ln_b[:, None, :]
        psi = jax.nn.gelu(psi, approximate=False)
        psi = jnp.einsum('tmg,tgo->tmo', psi, Wpsi2) + bpsi2[:, None, :]
        terms = phi * psi * temp_scale * mixing[:, None, None]
        ka = jnp.transpose(terms, (1, 0, 2)).reshape(Bx, H, 1, HD)
        enhanced_v = v * (1.0 + ka)
        out = jnp.einsum('bhnm,bhmd->bhnd', attn, enhanced_v)
        out = out.transpose(0, 2, 1, 3).reshape(Bx, Nx, Cx)
        return out @ Wproj + bproj

    def _L0_ffn_ref(x, router_kernel_DE, kernel_gating_EDF, kernel_up_EDF, kernel_down_EFD):
        import jax, jax.numpy as jnp
        import numpy as np
        TOP_K = 2
        E = router_kernel_DE.shape[-1]
        x = x.astype(jnp.float32)
        logits_BSE = jnp.einsum('BSD,DE->BSE', x, router_kernel_DE)
        probs_BSE = jax.nn.softmax(logits_BSE.astype(jnp.float32), axis=-1)
        weights_BSK, indices_BSK = jax.lax.top_k(probs_BSE, TOP_K)
        norm_weights_BSK = jax.nn.softmax(weights_BSK, axis=-1)
        one_hot_BSKE = jax.nn.one_hot(indices_BSK, num_classes=E, dtype=x.dtype)
        full_weights_BSE = jnp.sum(one_hot_BSKE * norm_weights_BSK[..., None], axis=2)
        gating_BSEF = jnp.einsum('BSD,EDF->BSEF', x, kernel_gating_EDF)
        act_BSEF = jax.nn.silu(gating_BSEF)
        up_BSEF = jnp.einsum('BSD,EDF->BSEF', x, kernel_up_EDF)
        fuse_BSEF = act_BSEF * up_BSEF
        down_BSED = jnp.einsum('BSEF,EFD->BSED', fuse_BSEF, kernel_down_EFD)
        out_BSD = jnp.einsum('BSED,BSE->BSD', down_BSED, full_weights_BSE)
        return out_BSD.astype(jnp.float32)

    def _L1_attn_ref(x, w_qkv, w_out, b_out):
        import jax, jax.numpy as jnp
        import numpy as np
        NUM_HEADS = 16

        def _stablemax3_s(x):
            pos = 1.0 + x * (1.0 + 0.5 * x * (1.0 + x / 3.0))
            neg = 1.0 / (1.0 - x * (1.0 - 0.5 * x * (1.0 - x / 3.0)))
            return jnp.where(x >= 0, pos, neg)

        def stablemax3(logits, axis=-1):
            logits = logits - jnp.max(logits, axis=axis, keepdims=True)
            s = _stablemax3_s(logits)
            return s / jnp.sum(s, axis=axis, keepdims=True)
        B, S, D = x.shape
        H = NUM_HEADS
        hd = D // H
        scale = hd ** (-0.5)
        qkv = x @ w_qkv.T
        qkv = qkv.reshape(B, S, 3, H, hd)
        qkv = jnp.transpose(qkv, (2, 0, 3, 1, 4))
        q, k, v = (qkv[0], qkv[1], qkv[2])
        attn = jnp.einsum('bhsd,bhtd->bhst', q, k) * scale
        attn = stablemax3(attn, axis=-1)
        out = jnp.einsum('bhst,bhtd->bhsd', attn, v)
        out = jnp.transpose(out, (0, 2, 1, 3)).reshape(B, S, D)
        return out @ w_out.T + b_out

    def _L1_ffn_ref(x, router_w, router_bias, gate_w, up_w, down_w, sgate_w, sup_w, sdown_w):
        import jax, jax.numpy as jnp
        import numpy as np
        TOPK = 4
        B, T, D = x.shape
        flat = x.reshape(B * T, D)
        logits = flat.astype(jnp.float32) @ router_w.T + router_bias
        scores = jax.nn.softmax(logits, axis=-1)
        topk_scores, topk_idx = jax.lax.top_k(scores, TOPK)
        topk_scores = topk_scores / jnp.clip(topk_scores.sum(axis=-1, keepdims=True), 1e-12, None)
        h = jax.nn.silu(jnp.einsum('nd,ehd->neh', flat, gate_w)) * jnp.einsum('nd,ehd->neh', flat, up_w)
        expert_out = jnp.einsum('neh,edh->ned', h, down_w)
        sel = jnp.take_along_axis(expert_out, topk_idx[:, :, None], axis=1)
        out = (sel * topk_scores.astype(flat.dtype)[:, :, None]).sum(axis=1)
        out = out + jax.nn.silu(flat @ sgate_w.T) * (flat @ sup_w.T) @ sdown_w.T
        return out.reshape(B, T, D)
    x = L0_attn_x
    mod = (_silu(L0_c) @ L0_wmod).reshape(L0_c.shape[0], 6, 1, -1)
    sa, ca, ga, sb, cb, gb = (mod[:, 0], mod[:, 1], mod[:, 2], mod[:, 3], mod[:, 4], mod[:, 5])
    ga = (2 * (ga >= 0) - 1) * jnp.maximum(jnp.abs(ga), 0.25)
    gb = (2 * (gb >= 0) - 1) * jnp.maximum(jnp.abs(gb), 0.25)
    h = _layernorm(x, axis=-1) * (1 + ca) + sa
    x = x + ga * _L0_attn_ref(h, L0_attn_Wqkv, L0_attn_Wproj, L0_attn_bproj, L0_attn_alpha, L0_attn_beta, L0_attn_gamma, L0_attn_A, L0_attn_Wphi1, L0_attn_bphi1, L0_attn_Wphi2, L0_attn_bphi2, L0_attn_Wpsi1, L0_attn_bpsi1, L0_attn_ln_g, L0_attn_ln_b, L0_attn_Wpsi2, L0_attn_bpsi2, L0_attn_mixing, L0_attn_temp_scale)
    h = _layernorm(x, axis=-1) * (1 + cb) + sb
    x = x + gb * _L0_ffn_ref(h, L0_ffn_router_kernel_DE, L0_ffn_kernel_gating_EDF, L0_ffn_kernel_up_EDF, L0_ffn_kernel_down_EFD)
    mod = (_silu(L1_c) @ L1_wmod).reshape(L1_c.shape[0], 6, 1, -1)
    sa, ca, ga, sb, cb, gb = (mod[:, 0], mod[:, 1], mod[:, 2], mod[:, 3], mod[:, 4], mod[:, 5])
    ga = (2 * (ga >= 0) - 1) * jnp.maximum(jnp.abs(ga), 0.25)
    gb = (2 * (gb >= 0) - 1) * jnp.maximum(jnp.abs(gb), 0.25)
    h = _layernorm(x, axis=-1) * (1 + ca) + sa
    x = x + ga * _L1_attn_ref(h, L1_attn_w_qkv, L1_attn_w_out, L1_attn_b_out)
    h = _layernorm(x, axis=-1) * (1 + cb) + sb
    x = x + gb * _L1_ffn_ref(h, L1_ffn_router_w, L1_ffn_router_bias, L1_ffn_gate_w, L1_ffn_up_w, L1_ffn_down_w, L1_ffn_sgate_w, L1_ffn_sup_w, L1_ffn_sdown_w)
    return x

_drawn_inputs = setup_inputs


def setup_inputs(seed=0):
    import zlib

    import numpy as np

    out = dict(_drawn_inputs(seed))
    spreads = {'L0_attn_bproj': (0.0, 0.279),
     'L0_attn_alpha': (1.0, 0.6),
     'L0_attn_beta': (1.0, 0.6),
     'L0_attn_gamma': (1.0, 0.6),
     'L0_attn_bphi1': (0.0, 0.8),
     'L0_attn_bphi2': (0.0, 0.8),
     'L0_attn_bpsi1': (0.0, 0.8),
     'L0_attn_ln_g': (1.0, 0.6),
     'L0_attn_ln_b': (0.0, 0.8),
     'L0_attn_bpsi2': (0.0, 0.8),
     'L0_attn_mixing': (0.25, 0.6),
     'L1_attn_b_out': (0.0, 0.303),
     'L1_ffn_router_bias': (0.0, 1.716)}
    factors = {'L0_attn_A': 8.0,
     'L0_attn_Wphi1': 8.0,
     'L0_attn_Wphi2': 8.0,
     'L0_attn_Wpsi1': 8.0,
     'L0_attn_Wpsi2': 8.0,
     'L0_ffn_router_kernel_DE': 8.0,
     'L0_ffn_kernel_gating_EDF': 8.0,
     'L0_ffn_kernel_up_EDF': 8.0,
     'L0_ffn_kernel_down_EFD': 8.0,
     'L1_attn_w_qkv': 8.0,
     'L1_attn_w_out': 8.0}
    for name, (base, spread) in spreads.items():
        noise = np.random.default_rng([zlib.crc32(name.encode()), seed]).standard_normal(out[name].shape)
        drawn = base * np.exp(spread * noise) if base else spread * noise
        out[name] = jnp.asarray(drawn.astype(out[name].dtype))
    for name, factor in factors.items():
        out[name] = (out[name] * factor).astype(out[name].dtype)
    return out
```

```python
from contextlib import ExitStack

import concourse.bass as bass
from concourse import mybir

F32 = mybir.dt.float32
F32R = mybir.dt.float32r
U32 = mybir.dt.uint32
ALU = mybir.AluOpType
ACT = mybir.ActivationFunctionType
AX = mybir.AxisListType

P = 128
NH = 16
HD = P // NH
HG = 4
NG = NH // HG
TOK = 512
NT = TOK // P
TEMPERATURE = 0.72
EPS = 1e-5
EXPERTS = [8, 32]
PER_EXPERT = [2, 1]
SHARED = [0, 4]
TOPK = [2, 4]
CHUNKS = [EXPERTS[l] * PER_EXPERT[l] + SHARED[l] for l in range(2)]
SHIFT_ROWS = 2
COPY0 = 8
M_SA, M_CA, M_GA, M_GAB, M_SB, M_CB, M_GB, M_PER = 0, 1, 2, 3, 4, 5, 6, 7
M_VAL = 14
M_COLS = 16

STEPS = 2 * NT
TLAG = STEPS + 4
PVLAG = [3, 5]
OLAG = 3
P_SLOTS = 3
KZ_SLOTS = 3

C_ID, C_ONES = 0, 128
C_LOQ, C_LOK, C_LOS, C_LOW, C_ONE2 = 256, 257, 258, 259, 260
C_HEAD = 264
C_RQ, C_RK = 280, 296
C_RT = 312
C_BM = 440
C_IOTA = 504
C_SEL = 536
C_COLS = 568
K_WQ, K_WK, K_P1, K_P2, K_A, K_PS1, K_PS2 = 0, 128, 256, 288, 296, 360, 424
K_BP1, K_BP2, K_BS1, K_G, K_B, K_BS2, K_MIX, K_TEMP, K_GAMMA = 432, 433, 434, 435, 436, 437, 438, 439, 440
K_BO = 441
K_C = 443
K_COLS = 459
A_Q, A_K, A_V, A_O, A_COLS = 0, 512, 1024, 1152, 1280


def bass_adaln_two_layers_kernel(nc, xT, attw, alpha, beta, modw, consts, kaw, ffg, ffu, ffd0, ffg1, ffu1, ffd1,
                                 router0, router1, rbias, outT):
    NB = xT.shape[0]
    ctx = ExitStack()
    with ctx:
        def sb(name, shape, dt=F32):
            return ctx.enter_context(nc.sbuf_tensor(name, shape, dt))

        def sem(name):
            return ctx.enter_context(nc.semaphore(name))

        x1T = nc.dram_tensor("x1T", [NB, P, TOK], F32, kind="Internal").ap()

        ps = ctx.enter_context(nc.psum_tensor("ps", [P, 8, TOK], F32))
        B_PV, B_MISC = 6, 7

        cst = sb("cst", [P, C_COLS])
        ident = cst[:, C_ID:C_ID + P]
        ones = cst[:, C_ONES:C_ONES + P]
        selr = sb("selr", [P, 32], F32R)
        kw = sb("kw", [P, K_COLS])
        aw = sb("aw", [P, A_COLS])
        bet = sb("bet", [P, NH])
        rw = [sb(f"rw{l}", [P, EXPERTS[l]]) for l in range(2)]
        rb = sb("rb", [P, EXPERTS[1]])
        MC = max(CHUNKS)
        whi = sb("whi", [P, 2, MC, P], F32R)
        wlo = sb("wlo", [P, 2, MC, P], F32R)
        wdn = sb("wdn", [P, MC, P])
        modb = sb("modb", [P, NB, M_COLS])
        mb = sb("mb", [P, M_COLS])
        sc = sb("sc", [P, 2, NB])
        mabs = sb("mabs", [P, 2, 2, NB])
        msgn = sb("msgn", [P, 2, 2, NB])
        hsum = sb("hsum", [P, NB])
        kd = sb("kd", [P, 2, NB, NH])

        x = sb("x", [P, TOK])
        h = sb("h", [P, TOK])
        pr = sb("pr", [P, P_SLOTS, HG, TOK])
        xc, sq, rs, hn = (pr[:, 0, n, :] for n in range(4))
        sil = pr[:, 1, 0:2, :]
        swt = pr[:, 1, 2:4, :]
        hid = pr[:, 2, 0:2, :]
        stage = pr[:, :, :, :].rearrange("p a b c -> p (a b c)")
        alph = stage[:, 3 * TOK:4 * TOK]
        qst = sb("qst", [P, NG, TOK], F32R)
        hhi, hlo, wst, wt = (qst[:, n, :] for n in range(4))
        kst = sb("kst", [P, NG, TOK])
        kt = kst[:, :, :].rearrange("p a (b c) -> p (a b) c", c=P)
        hit = sb("hit", [P, 2, TOK], F32R)
        kz = sb("kz", [P, KZ_SLOTS, HG, TOK], F32R)
        vx = sb("vx", [P, NT, NH, 32])
        mx = sb("mx", [P, NG, NT, HG])
        mxb = sb("mxb", [P, NT, HG])
        shc = sb("shc", [P, NT, P])
        sht = sb("sht", [P, TOK], F32R)
        shr = sb("shr", [P, TOK], F32R)
        o = sb("o", [P, TOK])
        orec = sb("orec", [P, NT, HG])
        a = sb("a", [P, NT, P])
        at = sb("at", [P, TOK])
        lg = sb("lg", [P, NT, 32])
        ex = sb("ex", [P, NT, 32])
        rsc = sb("rsc", [P, NT, 32])
        r1 = sb("r1", [P, NT])
        r2 = sb("r2", [P, NT])
        top = sb("top", [P, NT, 8])
        topi = sb("topi", [P, NT, 8], U32)
        topf = sb("topf", [P, NT, 8])
        eq = sb("eq", [P, NT, 32, 4])
        msk = sb("msk", [P, NT, 32])
        wd = sb("wd", [P, NT, P])

        c_in = sem("c_in")
        w_in = sem("w_in")
        g_in = sem("g_in")
        px_in = sem("px_in")
        zero_p = sem("zero_p")
        zero_v = sem("zero_v")
        ones_set = sem("ones_set")
        pdve = sem("pdve")
        pact = sem("pact")
        ppe = sem("ppe")
        lmean = sem("lmean")
        lcent = sem("lcent")
        lsq = sem("lsq")
        lvar = sem("lvar")
        llog = sem("llog")
        lrs = sem("lrs")
        lnorm = sem("lnorm")
        lh = sem("lh")
        lsum = sem("lsum")
        scaled = sem("scaled")
        N_CONST = 9

        block = ctx.enter_context(nc.Block())

        PE_MOD, PE_QM, PE_QK, PE_P1, PE_AX, PE_PS, PE_MU, PE_VAR, PE_PH, PE_PSI, PE_KA = range(1, 12)
        ACT_SILU, ACT_ABS, ACT_PH1, ACT_VAR, ACT_RS, ACT_GELU = range(1, 7)

        D_HM, D_KD, D_QK, D_AX, D_PS, D_SQ, D_LNG, D_TERM, D_ALL = (
            PRE["hm"], PRE["kd"], PRE["qk"], PRE["ax"], PRE["psi"], PRE["sq"], PRE["lng"], PRE["term"], PRE["all"])

        def sems(l):
            names = ("x_in x_out mbr mean cent sqd var logv rstd norm hr stk_mm stk_t stk_r kzr s_mm s_red "
                     "sh_b sh_c sh_mm sh_t sh_r sh_q st_mm sq_p y_p ln_p p_r pv o_c o_tr o_rc o_n a_tr a_ev proj xa1 xa2 "
                     "hhir hlor rt_mm rt_d rt_e w_c w_tr w_t w_r wb g_mm u_mm sil_r t_r h_r dn xf").split()
            return {n: sem(f"{n}{l}") for n in names}

        S = [sems(0), sems(1)]
        wsp = [sem("wsp0"), sem("wsp1")]
        wspd = [sem("wspd0"), sem("wspd1")]
        wstg = [[sem(f"wstg{l}_{n}") for n in range(4)] for l in range(2)]

        ffw = [(ffg, ffu, ffd0), (ffg1, ffu1, ffd1)]
        PIECE = 12

        def pieces(l):
            return [(m, c0, min(PIECE, CHUNKS[l] - c0)) for m in range(2) for c0 in range(0, CHUNKS[l], PIECE)]

        STG = 4 * PIECE * P

        def staged(n, k):
            return stage[:, (n % 4) * PIECE * P:(n % 4) * PIECE * P + k * P]

        srcx = [xT, x1T]
        dstx = [x1T, outT]

        STK = [("k", 0), ("q", 0), ("v", 0)] + [(w, t) for t in range(1, NG) for w in "kq"]
        STK_K = [STK.index(("k", t)) for t in range(NG)]
        STK_Q = [STK.index(("q", t)) for t in range(NG)]
        SPLITS = [n for n, (w, _) in enumerate(STK) if w != "v"]

        @block.sync
        def _(sp):
            sp.dma_start(cst[:, :], consts).then_inc(c_in, 16)
            sp.dma_start(kw[:, :], kaw).then_inc(c_in, 16)
            for l in range(2):
                sp.dma_start(stage[:, l * 768:(l + 1) * 768], modw[l]).then_inc(c_in, 16)
            sp.dma_start(aw[:, :], attw[0]).then_inc(c_in, 16)
            sp.dma_start(alph, alpha.partition_broadcast(P)).then_inc(c_in, 16)
            sp.dma_start(bet[:, :], beta.partition_broadcast(P)).then_inc(c_in, 16)
            sp.dma_start(rw[0][:, :], router0).then_inc(c_in, 16)
            sp.dma_start(rw[1][:, :], router1).then_inc(c_in, 16)
            sp.dma_start(rb[:, :], rbias.partition_broadcast(P)).then_inc(w_in, 16)
            with sp.Fori(0, NB) as i:
                sp.wait_ge(lcent, i)
                sp.dma_start(x[:, :], xT[i, :, :]).then_inc(px_in, 16)
            for l in range(2):
                if l == 0:
                    sp.wait_ge(ppe, PE_MOD)
                    sp.wait_ge(lh, 2 * NB)
                else:
                    sp.wait_ge(S[0]["xf"], NB)
                    sp.dma_start(aw[:, :], attw[1]).then_inc(w_in, 16)
                for n, (m, c0, k) in enumerate(pieces(l)):
                    if n >= 4:
                        sp.wait_ge(wsp[l], n - 3)
                        sp.wait_ge(wspd[l], n - 3)
                    sp.dma_start(staged(n, k), ffw[l][m][:, c0 * P:(c0 + k) * P]).then_inc(wstg[l][n % 4], 16)
                sp.dma_start(wdn[:, 0:CHUNKS[l], :].rearrange("p a b -> p (a b)"), ffw[l][2]).then_inc(g_in, 16)
                with sp.Fori(0, NB) as i:
                    sp.wait_ge(S[l]["x_out"], i * 16)
                    if l == 0:
                        sp.wait_ge(lcent, NB)
                    sp.dma_start(x[:, :], srcx[l][i, :, :]).then_inc(S[l]["x_in"], 16)
                    sp.wait_ge(S[l]["xf"], i + 1)
                    sp.dma_start(dstx[l][i, :, :], x[:, :]).then_inc(S[l]["x_out"], 16)
                sp.wait_ge(S[l]["x_out"], NB * 16)

        @block.gpsimd
        def _(pool):
            s0 = nc.gpsimd.memset(kz[:, :, :, :].bitcast(F32).rearrange("p a b c -> p (a b c)"), 0.0)
            s0.then_inc(zero_p, 1)
            nc.gpsimd.memset(vx[:, :, :, :], 0.0).then_inc(zero_p, 1)
            pool.wait_ge(zero_p, 2)
            nc.gpsimd.memset(vx[:, :, :, HD:HD + 1], 1.0).then_inc(ones_set, 1)
            nc.gpsimd.memset(shc[:, :, :], 0.0).then_inc(ones_set, 1)
            nc.gpsimd.memset(wd[:, :, :], 0.0).then_inc(ones_set, 1)
            for l in range(2):
                s = S[l]
                with pool.Fori(0, NB) as i:
                    def scatter(t):
                        if t == 0:
                            pool.wait_ge(s["sh_q"], i * 4)
                        elif t == 3:
                            pool.wait_ge(s["sh_q"], i * 4 + 1)
                        pool.wait_ge(s["stk_r"], i * 9 + STK_K[t] + 1)
                        if t < KZ_SLOTS:
                            pool.wait_ge(s["st_mm"], i * 32)
                        else:
                            pool.wait_ge(s["st_mm"], i * 32 + 8 * (t - KZ_SLOTS + 1))
                        pool.nop(nofuse=True)
                        for j in range(HG):
                            q = slice(32 * j, 32 * j + 32)
                            nc.gpsimd.tensor_copy(kz[q, t % KZ_SLOTS, j, :],
                                                  kst[q, t, :].bitcast(F32)).then_inc(s["kzr"], 1)

                    def shift(t):
                        pool.wait_ge(s["kzr"], i * 16 + (4 * KZ_SLOTS if t == 0 else 4 * NG))
                        pool.wait_ge(s["sh_r"], i * 4 + t + 1)
                        nc.gpsimd.tensor_tensor(qst[:, t, :], qst[:, t, :].bitcast(F32), shr[:, :].bitcast(F32),
                                                ALU.add).then_inc(s["sh_q"], 1)

                    for t in range(KZ_SLOTS):
                        scatter(t)
                    shift(0)
                    scatter(3)
                    for t in range(1, NG):
                        shift(t)

        def each_step(l):
            last = 8 * NG + TLAG + PVLAG[l] + OLAG + 8
            for g in range(last):
                ev = []
                if g < 8 * NG:
                    ev.append(("s", g))
                for t in range(NG):
                    if g == 8 * (t + 1) + 1:
                        ev.append(("shift", t))
                u = g - TLAG
                if 0 <= u < 8 * NG:
                    ev.append(("st", u))
                v = u - PVLAG[l]
                if v >= 0 and v % 2 == 0 and v // 2 < NG * NT:
                    ev.append(("pv", v // 2))
                w = v - 2 * (NT - 1) - OLAG
                if w >= 0 and w % 8 == 0 and w // 8 < NG:
                    ev.append(("out", w // 8))
                yield ev

        def before(l, kind, n, other):
            order = [e for ev in each_step(l) for e in ev]
            return sum(k == other for k, _ in order[:order.index((kind, n))])

        @block.tensor
        def _(pe):
            mm = nc.tensor.matmul
            pe.wait_ge(c_in, 16 * N_CONST)
            pe.wait_ge(pact, ACT_SILU)
            for l in range(2):
                for j in range(6):
                    last = mm(ps[:, 0, (l * 6 + j) * NB:(l * 6 + j + 1) * NB],
                              stage[:, l * 768 + j * P:l * 768 + (j + 1) * P], sc[:, l, :], start=True, stop=True)
            last.then_inc(ppe, 1)
            with pe.Fori(0, NB) as i:
                pe.wait_ge(px_in, i * 16 + 16)
                pe.wait_ge(lcent, i)
                mm(ps[:, 6, :], ones, x[:, :], start=True, stop=True).then_inc(lmean, 1)
                pe.wait_ge(lsq, i + 1)
                pe.wait_ge(llog, i)
                mm(ps[:, 7, :], ones, sq, start=True, stop=True).then_inc(lvar, 1)
            pe.wait_ge(pdve, D_HM)
            mm(ps[:, 1, 0:NB], kw[:, K_WQ:K_WQ + P], hsum[:, :], start=True, stop=True)
            mm(ps[:, 1, NB:2 * NB], kw[:, K_WK:K_WK + P], hsum[:, :], start=True, stop=True).then_inc(ppe, 1)
            pe.wait_ge(pdve, D_KD)
            for n, c in enumerate((C_RQ, C_RK)):
                last = mm(ps[0:16, 2, 0:P], cst[:, c:c + 16], kd[:, n, :, :].rearrange("p a b -> p (a b)"),
                          start=(n == 0), stop=(n == 1))
            last.then_inc(ppe, 1)
            pe.wait_ge(pdve, D_QK)
            mm(ps[0:32, 3, 0:P], kw[0:16, K_P1:K_P1 + 32], kt[0:16, 0, :], start=True, stop=True).then_inc(ppe, 1)
            mm(ps[0:64, 4, 0:P], kw[0:16, K_A:K_A + 64], kt[0:16, 0, :], start=True, stop=True).then_inc(ppe, 1)
            pe.wait_ge(pdve, D_AX)
            mm(ps[0:64, 5, 0:P], kw[0:64, K_PS1:K_PS1 + 64], kt[0:64, 1, :], start=True, stop=True).then_inc(ppe, 1)
            pe.wait_ge(pdve, D_PS)
            mm(ps[0:64, 4, 0:P], cst[0:64, C_BM:C_BM + 64], kt[0:64, 2, :], start=True, stop=True).then_inc(ppe, 1)
            pe.wait_ge(pdve, D_SQ)
            mm(ps[0:64, 5, 0:P], cst[0:64, C_BM:C_BM + 64], kt[0:64, 4, :], start=True, stop=True).then_inc(ppe, 1)
            pe.wait_ge(pact, ACT_PH1)
            mm(ps[0:8, 2, 0:P], kw[0:32, K_P2:K_P2 + 8], kt[0:32, 5, :], start=True, stop=True).then_inc(ppe, 1)
            pe.wait_ge(pact, ACT_GELU)
            mm(ps[0:8, 3, 0:P], kw[0:64, K_PS2:K_PS2 + 8], kt[0:64, 9, :], start=True, stop=True).then_inc(ppe, 1)
            pe.wait_ge(pdve, D_TERM)
            mm(ps[:, 4, 0:P], cst[0:8, C_RT:C_RT + P], kt[0:8, 12, :], start=True, stop=True).then_inc(ppe, 1)
            pe.wait_ge(ones_set, 3)

            for l in range(2):
                s = S[l]
                w = aw
                if l == 1:
                    pe.wait_ge(w_in, 32)
                E, NCH = EXPERTS[l], CHUNKS[l]
                with pe.Fori(0, NB) as i:
                    def norm(k):
                        if k == 0:
                            pe.wait_ge(s["x_in"], i * 16 + 16)
                        else:
                            pe.wait_ge(s["xa2"], i + 1)
                        mm(ps[:, B_PV, :], ones, x[:, :], start=True, stop=True).then_inc(s["mean"], 1)
                        pe.wait_ge(s["sqd"], i * 2 + k + 1)
                        mm(ps[:, B_MISC, :], ones, sq, start=True, stop=True).then_inc(s["var"], 1)

                    norm(0)
                    if l == 0:
                        pe.wait_ge(pdve, D_ALL)
                    else:
                        pe.wait_ge(scaled, 1)
                    pe.wait_ge(s["hr"], i * 2 + 1)
                    for n, (kind, t) in enumerate(STK):
                        if n >= 6:
                            pe.wait_ge(s["stk_r"], i * 9 + n - 5)
                        if kind == "v":
                            for q in range(NT):
                                last = mm(ps[:, n % 6, q * P:(q + 1) * P], h[:, q * P:(q + 1) * P],
                                          w[:, A_V:A_V + P], start=True, stop=True)
                            last.then_inc(s["stk_mm"], 1)
                        else:
                            c = (A_K if kind == "k" else A_Q) + t * P
                            mm(ps[:, n % 6, :], w[:, c:c + P], h[:, :], start=True, stop=True)\
                                .then_inc(s["stk_mm"], 1)
                    for ev in each_step(l):
                        for kind, n in ev:
                            if kind == "s":
                                t, q, jp = n // 8, n % 8 // 2, n % 2
                                if n == 0:
                                    pe.wait_ge(s["stk_r"], i * 9 + 9)
                                if n % 8 == 0:
                                    pe.wait_ge(s["kzr"], i * 16 + 4 * t + 4)
                                if n >= 1:
                                    pe.wait_ge(s["s_red"], i * 32 + n)
                                for j in range(2):
                                    last = mm(ps[:, j, :], qst[:, t, q * P:(q + 1) * P],
                                              kz[:, t % KZ_SLOTS, 2 * jp + j, :], start=True, stop=True)
                                last.then_inc(s["s_mm"], 1)
                            elif kind == "shift":
                                pe.wait_ge(s["sh_c"], i * 4 + n + 1)
                                if before(l, kind, n, "out"):
                                    pe.wait_ge(s["o_n"], i * 4 + before(l, kind, n, "out"))
                                if n >= 1:
                                    pe.wait_ge(s["sh_r"], i * 4 + n)
                                for q in range(NT):
                                    last = nc.tensor.transpose(ps[:, B_MISC, q * P:(q + 1) * P], shc[:, q, :], ident)
                                last.then_inc(s["sh_mm"], 1)
                            elif kind == "st":
                                t, k, jp = n // 8, n % 8 // 2, n % 2
                                if n % 8 == 0:
                                    pe.wait_ge(s["sh_q"], i * 4 + t + 1)
                                if n >= 2:
                                    pe.wait_ge(s["p_r"] if l == 0 else s["y_p"], i * 32 + n - 1)
                                for j in range(2):
                                    last = mm(ps[:, 2 + 2 * (n % 2) + j, :],
                                              kz[:, t % KZ_SLOTS, 2 * jp + j, k * P:(k + 1) * P],
                                              qst[:, t, :], start=True, stop=True)
                                last.then_inc(s["st_mm"], 1)
                            elif kind == "pv":
                                t, k = n // NT, n % NT
                                pe.wait_ge(s["p_r"], i * 32 + 2 * n + 2 if l == 0 else i * 16 + n + 1)
                                if k == 0 and t > 0:
                                    pe.wait_ge(s["o_c"], i * 4 + t)
                                for j in range(HG):
                                    last = mm(ps[32 * j:32 * j + 32, B_PV, :], vx[:, k, HG * t + j, :],
                                              pr[:, n % P_SLOTS, j, :], start=(k == 0), stop=(k == NT - 1))
                                last.then_inc(s["pv"], 1)
                            else:
                                pe.wait_ge(s["o_c"], i * 4 + n + 1)
                                pe.wait_ge(s["sh_r"], i * 4 + before(l, kind, n, "shift"))
                                if n >= 1:
                                    pe.wait_ge(s["o_n"], i * 4 + n)
                                for q in range(NT):
                                    last = nc.tensor.transpose(ps[:, B_MISC, q * P:(q + 1) * P],
                                                               o[:, q * P:(q + 1) * P], ident)
                                last.then_inc(s["o_tr"], 1)
                    pe.wait_ge(s["o_n"], i * 4 + 4)
                    for q in range(NT):
                        last = nc.tensor.transpose(ps[:, B_MISC, q * P:(q + 1) * P], a[:, q, :], ident)
                    last.then_inc(s["a_tr"], 1)
                    pe.wait_ge(s["a_ev"], i + 1)
                    mm(ps[:, 0, :], w[:, A_O:A_O + P], at[:, :], start=True, stop=True).then_inc(s["proj"], 1)

                    norm(1)
                    pe.wait_ge(s["hr"], i * 2 + 2)
                    for q in range(NT):
                        last = mm(ps[:, 0, q * E:(q + 1) * E], h[:, q * P:(q + 1) * P], rw[l][:, :],
                                  start=True, stop=True)
                    last.then_inc(s["rt_mm"], 1)
                    pe.wait_ge(s["w_c"], i + 1)
                    for q in range(NT):
                        last = nc.tensor.transpose(ps[:, B_MISC, q * P:(q + 1) * P], wd[:, q, :], ident)
                    last.then_inc(s["w_tr"], 1)
                    pe.wait_ge(s["hhir"], i + 1)
                    pe.wait_ge(s["hlor"], i + 1)
                    pe.wait_ge(wsp[l], len(pieces(l)))
                    pe.wait_ge(wspd[l], len(pieces(l)))
                    pe.wait_ge(g_in, 16 * (l + 1))

                    def down(c):
                        pe.wait_ge(s["h_r"], i * NCH + c + 1)
                        mm(ps[:, B_PV, :], wdn[:, c, :], hid[:, c % 2, :], start=(c == 0), stop=(c == NCH - 1))\
                            .then_inc(s["dn"], 1)

                    for c in range(NCH):
                        e = c // PER_EXPERT[l]
                        for m, bank, name in ((0, 0, "g_mm"), (1, 2, "u_mm")):
                            if c >= 2:
                                pe.wait_ge(s["sil_r" if m == 0 else "h_r"], i * NCH + c - 1)
                            b = ps[:, bank + c % 2, :]
                            mm(b, wlo[:, m, c, :], hhi, start=True, stop=False)
                            mm(b, whi[:, m, c, :], hlo, start=False, stop=False)
                            mm(b, whi[:, m, c, :], hhi, start=False, stop=True).then_inc(s[name], 1)
                            if m == 0 and c % PER_EXPERT[l] == 0 and e < E:
                                if e == 0:
                                    pe.wait_ge(s["w_r"], i + 1)
                                if e >= 2:
                                    pe.wait_ge(s["t_r"], i * E * PER_EXPERT[l] + (e - 1) * PER_EXPERT[l])
                                mm(ps[:, 4 + e % 2, :], selr[:, e:e + 1].to_broadcast([P, P]), wst,
                                   start=True, stop=True).then_inc(s["wb"], 1)
                        if c >= 1:
                            down(c - 1)
                    down(NCH - 1)

        @block.scalar
        def _(act):
            act.preload_act_table_set("silu_and_others")
            act.wait_ge(c_in, 16 * N_CONST)
            nc.scalar.activation(sc[:, :, :], kw[:, K_C:K_C + 2 * NB].rearrange("p (a b) -> p a b", a=2),
                                 ACT.Silu).then_inc(pact, 1)
            act.wait_ge(ppe, PE_MOD)
            for g in range(2):
                last = nc.scalar.activation(mabs[:, :, g, :],
                                            ps[:, 0, 0:12 * NB].rearrange("p (a b c) -> p a b c", a=2, b=6)[
                                                :, :, 2 + 3 * g, :], ACT.Abs)
            last.then_inc(pact, 1)
            act.preload_act_table_set("natural_log_exp_and_others")
            with act.Fori(0, NB) as i:
                act.wait_ge(lcent, i + 1)
                nc.scalar.activation(sq, xc, ACT.Square).then_inc(lsq, 1)
                act.wait_ge(lvar, i + 1)
                nc.scalar.activation(rs, ps[:, 7, :], ACT.Ln, bias=cst[:, C_ONE2 + 1:C_ONE2 + 2]).then_inc(llog, 1)
                act.wait_ge(llog, i + 1)
                nc.scalar.activation(rs, rs, ACT.Exp, scale=-0.5).then_inc(lrs, 1)
            act.wait_ge(ppe, PE_P1)
            nc.scalar.activation(kt[0:32, 5, :], ps[0:32, 3, 0:P], ACT.Silu,
                                 bias=kw[0:32, K_BP1:K_BP1 + 1]).then_inc(pact, 1)
            act.wait_ge(ppe, PE_VAR)
            nc.scalar.activation(kt[0:64, 6, :], ps[0:64, 5, 0:P], ACT.Ln,
                                 bias=cst[0:64, C_ONE2 + 1:C_ONE2 + 2]).then_inc(pact, 1)
            act.wait_ge(pact, ACT_VAR)
            nc.scalar.activation(kt[0:64, 7, :], kt[0:64, 6, :], ACT.Exp, scale=-0.5).then_inc(pact, 1)
            act.wait_ge(pdve, D_LNG)
            nc.scalar.activation(kt[0:64, 9, :], kt[0:64, 8, :], ACT.Gelu).then_inc(pact, 1)

            for l in range(2):
                s = S[l]
                NCH = CHUNKS[l]
                for n, (m, c0, k) in enumerate(pieces(l)):
                    act.wait_ge(wstg[l][n % 4], 16 * (n // 4) + 16)
                    nc.scalar.activation(whi[:, m, c0:c0 + k, :].rearrange("p a b -> p (a b)"), staged(n, k),
                                         ACT.Copy).then_inc(wsp[l], 1)
                with act.Fori(0, NB) as i:
                    def norm(k):
                        act.wait_ge(s["cent"], i * 2 + k + 1)
                        nc.scalar.activation(sq, xc, ACT.Square).then_inc(s["sqd"], 1)
                        act.wait_ge(s["var"], i * 2 + k + 1)
                        nc.scalar.activation(rs, ps[:, B_MISC, :], ACT.Ln,
                                             bias=cst[:, C_ONE2 + 1:C_ONE2 + 2]).then_inc(s["logv"], 1)
                        act.wait_ge(s["logv"], i * 2 + k + 1)
                        nc.scalar.activation(rs, rs, ACT.Exp, scale=-0.5).then_inc(s["rstd"], 1)

                    act.preload_act_table_set("natural_log_exp_and_others")
                    norm(0)
                    for m, n in enumerate(SPLITS):
                        act.wait_ge(s["stk_mm"], i * 9 + n + 1)
                        if m >= 2:
                            act.wait_ge(s["stk_r"], i * 9 + SPLITS[m - 2] + 1)
                        lo = cst[:, C_LOK:C_LOK + 1] if STK[n][0] == "k" else cst[:, C_LOQ:C_LOQ + 1]
                        nc.scalar.activation(hit[:, m % 2, :], ps[:, n % 6, :], ACT.Copy, scale=lo)\
                            .then_inc(s["stk_t"], 1)

                    def recip(n):
                        act.wait_ge(s["y_p"], i * 32 + 2 * n + 2)
                        v = pr[:, n % P_SLOTS, :, :]
                        nc.scalar.activation(v, v, ACT.Ln, scale=-1.0 / 6.0, bias=cst[:, C_ONE2 + 2:C_ONE2 + 3])\
                            .then_inc(s["ln_p"], 1)
                        act.wait_ge(s["ln_p"], i * 16 + n + 1)
                        nc.scalar.activation(v, v, ACT.Exp, scale=-1.0).then_inc(s["p_r"], 1)

                    for ev in each_step(l):
                        for kind, n in ev:
                            if kind == "shift":
                                act.wait_ge(s["sh_mm"], i * 4 + n + 1)
                                nc.scalar.activation(sht[:, :], ps[:, B_MISC, :], ACT.Copy,
                                                     scale=cst[:, C_LOS:C_LOS + 1]).then_inc(s["sh_t"], 1)
                            elif kind == "st":
                                act.wait_ge(s["st_mm"], i * 32 + n + 1)
                                slot = n // 2
                                if slot >= P_SLOTS and n % 2 == 0:
                                    act.wait_ge(s["pv"], i * 16 + slot - P_SLOTS + 1)
                                dst = pr[:, slot % P_SLOTS, 2 * (n % 2):2 * (n % 2) + 2, :]
                                src = ps[:, 2 + 2 * (n % 2):4 + 2 * (n % 2), :]
                                if l == 0:
                                    nc.scalar.activation(dst, src, ACT.Exp).then_inc(s["p_r"], 1)
                                else:
                                    nc.scalar.activation(dst, src, ACT.Square).then_inc(s["sq_p"], 1)
                                    if n % 2 and n >= 3:
                                        recip(n // 2 - 1)
                            elif kind == "pv" and n % NT == NT - 1:
                                if l == 1 and n == NG * NT - 1:
                                    recip(n)
                                t = n // NT
                                act.wait_ge(s["pv"], i * 16 + n + 1)
                                if t >= 1:
                                    act.wait_ge(s["o_tr"], i * 4 + t)
                                nc.scalar.activation(o[:, :], ps[:, B_PV, :], ACT.Copy).then_inc(s["o_c"], 1)
                    act.wait_ge(s["a_tr"], i + 1)
                    if l == 0:
                        nc.scalar.activation(at[:, :], ps[:, B_MISC, :], ACT.Copy, scale=mb[:, M_VAL:M_VAL + 1])\
                            .then_inc(s["a_ev"], 1)
                    else:
                        nc.scalar.activation(at[:, :], ps[:, B_MISC, :], ACT.Copy).then_inc(s["a_ev"], 1)

                    norm(1)
                    act.wait_ge(s["norm"], i * 2 + 2)
                    nc.scalar.activation(hhi, hn, ACT.Identity, scale=mb[:, l * M_PER + M_CB:l * M_PER + M_CB + 1],
                                         bias=mb[:, l * M_PER + M_SB:l * M_PER + M_SB + 1]).then_inc(s["hhir"], 1)
                    E = EXPERTS[l]
                    act.wait_ge(s["rt_d"], i * RT_N[l] + RT_EXP)
                    nc.scalar.activation(ex[:, :, 0:E], lg[:, :, 0:E], ACT.Exp).then_inc(s["rt_e"], 1)
                    if l == 0:
                        act.wait_ge(s["rt_d"], i * RT_N[l] + RT_EXP2)
                        nc.scalar.activation(ex[:, :, 0:E], lg[:, :, 0:E], ACT.Exp).then_inc(s["rt_e"], 1)
                    act.wait_ge(s["w_tr"], i + 1)
                    nc.scalar.activation(wt, ps[:, B_MISC, :], ACT.Copy, scale=cst[:, C_LOW:C_LOW + 1])\
                        .then_inc(s["w_t"], 1)
                    act.preload_act_table_set("silu_and_others")
                    for c in range(NCH):
                        act.wait_ge(s["g_mm"], i * NCH + c + 1)
                        if c >= 2:
                            if c - 2 < E * PER_EXPERT[l]:
                                act.wait_ge(s["t_r"], i * E * PER_EXPERT[l] + c - 1)
                            else:
                                act.wait_ge(s["h_r"], i * NCH + c - 1)
                        nc.scalar.activation(sil[:, c % 2, :], ps[:, c % 2, :], ACT.Silu).then_inc(s["sil_r"], 1)

        @block.vector
        def _(dve):
            ve = nc.vector
            count = [0]

            def link(ins, name=None):
                count[0] += 1
                ins.then_inc(pdve, 1)
                dve.wait_ge(pdve, count[0])
                if name:
                    assert PRE[name] == count[0], (name, count[0])

            dve.wait_ge(c_in, 16 * N_CONST)
            link(ve.tensor_copy(selr[:, :], cst[:, C_SEL:C_SEL + 32]))
            link(ve.scalar_tensor_tensor(out=aw[:, A_Q:A_Q + 512], in0=aw[:, A_Q:A_Q + 512],
                                         scalar=float(HD) ** -0.5 / TEMPERATURE, in1=alph,
                                         op0=ALU.mult, op1=ALU.mult))
            dve.wait_ge(pact, ACT_ABS)
            for l in range(2):
                mp = ps[:, 0, l * 6 * NB:(l + 1) * 6 * NB].rearrange("p (a b) -> p b a", a=6)
                for g in range(2):
                    o0 = l * M_PER + (M_SA if g == 0 else M_SB)
                    link(ve.tensor_copy(modb[:, :, o0], mp[:, :, 3 * g]))
                    link(ve.tensor_scalar(modb[:, :, o0 + 1], mp[:, :, 3 * g + 1], 1.0, None, ALU.add))
                    link(ve.tensor_scalar(msgn[:, l, g, :], mp[:, :, 3 * g + 2], 0.0, 2.0, ALU.is_ge, ALU.mult))
                    link(ve.tensor_scalar(mabs[:, l, g, :], mabs[:, l, g, :], 0.25, None, ALU.max))
                    link(ve.scalar_tensor_tensor(out=modb[:, :, o0 + 2], in0=msgn[:, l, g, :], scalar=-1.0,
                                                 in1=mabs[:, l, g, :], op0=ALU.add, op1=ALU.mult))
                o0 = l * M_PER
                link(ve.tensor_scalar(modb[:, :, o0 + M_GAB], modb[:, :, o0 + M_GA], kw[:, K_BO + l:K_BO + l + 1],
                                      None, ALU.mult))
            with dve.Fori(0, NB) as i:
                dve.wait_ge(lmean, i + 1)
                dve.wait_ge(lnorm, i)
                ve.tensor_tensor(xc, x[:, :], ps[:, 6, :], ALU.subtract).then_inc(lcent, 1)
                ve.tensor_copy(mb[:, 0:M_VAL], modb[:, bass.ds(i, 1), 0:M_VAL].rearrange("p a b -> p (a b)")).then_inc(lh, 1)
                dve.wait_ge(lcent, i + 1)
                dve.wait_ge(lrs, i + 1)
                ve.tensor_tensor(hn, xc, rs, ALU.mult).then_inc(lnorm, 1)
                dve.wait_ge(lnorm, i + 1)
                dve.wait_ge(lh, 2 * i + 1)
                ve.tensor_scalar(h[:, :], hn, mb[:, M_CA:M_CA + 1], mb[:, M_SA:M_SA + 1], ALU.mult, ALU.add)\
                    .then_inc(lh, 1)
                dve.wait_ge(lh, 2 * i + 2)
                ve.tensor_reduce(hsum[:, bass.ds(i, 1)], h[:, :], AX.X, ALU.add).then_inc(lsum, 1)
            dve.wait_ge(lsum, NB)
            link(ve.tensor_scalar(hsum[:, :], hsum[:, :], 1.0 / TOK, None, ALU.mult), "hm")
            dve.wait_ge(ppe, PE_QM)
            head = cst[:, C_HEAD:C_HEAD + NH].unsqueeze(1).to_broadcast([P, NB, NH])
            for n in range(2):
                link(ve.tensor_tensor(kd[:, n, :, :], head,
                                      ps[:, 1, n * NB:(n + 1) * NB].unsqueeze(2).to_broadcast([P, NB, NH]), ALU.mult),
                     "kd" if n else None)
            dve.wait_ge(ppe, PE_QK)
            link(ve.tensor_copy(kt[0:16, 0, :], ps[0:16, 2, 0:P]), "qk")
            dve.wait_ge(ppe, PE_AX)
            link(ve.tensor_copy(kt[0:64, 1, :], ps[0:64, 4, 0:P]), "ax")
            dve.wait_ge(ppe, PE_PS)
            link(ve.tensor_scalar(kt[0:64, 2, :], ps[0:64, 5, 0:P], kw[0:64, K_BS1:K_BS1 + 1], None, ALU.add), "psi")
            dve.wait_ge(ppe, PE_MU)
            link(ve.tensor_tensor(kt[0:64, 3, :], kt[0:64, 2, :], ps[0:64, 4, 0:P], ALU.subtract))
            link(ve.tensor_tensor(kt[0:64, 4, :], kt[0:64, 3, :], kt[0:64, 3, :], ALU.mult), "sq")
            dve.wait_ge(pact, ACT_RS)
            link(ve.tensor_tensor(kt[0:64, 13, :], kt[0:64, 3, :], kt[0:64, 7, :], ALU.mult))
            link(ve.tensor_scalar(kt[0:64, 8, :], kt[0:64, 13, :], kw[0:64, K_G:K_G + 1], kw[0:64, K_B:K_B + 1],
                                  ALU.mult, ALU.add), "lng")
            dve.wait_ge(ppe, PE_PH)
            link(ve.tensor_scalar(kt[0:8, 10, :], ps[0:8, 2, 0:P], kw[0:8, K_BP2:K_BP2 + 1], None, ALU.add))
            dve.wait_ge(ppe, PE_PSI)
            link(ve.scalar_tensor_tensor(out=kt[0:8, 11, :], in0=ps[0:8, 3, 0:P], scalar=kw[0:8, K_BS2:K_BS2 + 1],
                                         in1=kt[0:8, 10, :], op0=ALU.add, op1=ALU.mult))
            link(ve.tensor_scalar(kt[0:8, 12, :], kt[0:8, 11, :], kw[0:8, K_TEMP:K_TEMP + 1],
                                  kw[0:8, K_MIX:K_MIX + 1], ALU.mult, ALU.mult), "term")
            dve.wait_ge(ppe, PE_KA)
            link(ve.tensor_tensor(kd[:, 0, :, :], head,
                                  ps[:, 4, 0:P].rearrange("p (a b) -> p a b", b=NH), ALU.mult))
            link(ve.tensor_reduce(hsum[:, :], kd[:, 0, :, :], AX.X, ALU.add))
            link(ve.tensor_scalar(modb[:, :, M_VAL], hsum[:, :], 1.0, kw[:, K_GAMMA:K_GAMMA + 1], ALU.add, ALU.mult),
                 "all")
            dve.wait_ge(ones_set, 3)

            for l in range(2):
                s = S[l]
                E, NCH = EXPERTS[l], CHUNKS[l]
                EC = E * PER_EXPERT[l]
                if l == 1:
                    dve.wait_ge(w_in, 32)
                    ve.tensor_scalar(aw[:, A_Q:A_Q + 512], aw[:, A_Q:A_Q + 512], float(HD) ** -0.5, None,
                                     ALU.mult).then_inc(scaled, 1)
                for n, (m, c0, k) in enumerate(pieces(l)):
                    dve.wait_ge(wsp[l], n + 1)
                    part = whi[:, m, c0:c0 + k, :].rearrange("p a b -> p (a b)").bitcast(F32)
                    ve.tensor_tensor(wlo[:, m, c0:c0 + k, :].rearrange("p a b -> p (a b)"), staged(n, k), part,
                                     ALU.subtract).then_inc(wspd[l], 1)
                dve.wait_ge(wspd[l], len(pieces(l)))
                dve.wait_ge(wsp[l], len(pieces(l)))
                with dve.Fori(0, NB) as i:
                    dve.wait_ge(s["xf"], i)
                    ve.tensor_copy(mb[:, 0:M_VAL + 1], modb[:, bass.ds(i, 1), 0:M_VAL + 1].rearrange("p a b -> p (a b)"))\
                        .then_inc(s["mbr"], 1)

                    def norm(k):
                        dve.wait_ge(s["mean"], i * 2 + k + 1)
                        ve.tensor_tensor(xc, x[:, :], ps[:, B_PV, :], ALU.subtract).then_inc(s["cent"], 1)
                        dve.wait_ge(s["cent"], i * 2 + k + 1)
                        dve.wait_ge(s["rstd"], i * 2 + k + 1)
                        ve.tensor_tensor(hn, xc, rs, ALU.mult).then_inc(s["norm"], 1)
                        dve.wait_ge(s["norm"], i * 2 + k + 1)
                        dve.wait_ge(s["mbr"], i + 1)
                        o0 = l * M_PER + (M_SA if k == 0 else M_SB)
                        ve.tensor_scalar(h[:, :], hn, mb[:, o0 + 1:o0 + 2], mb[:, o0:o0 + 1], ALU.mult, ALU.add)\
                            .then_inc(s["hr"], 1)

                    norm(0)
                    for n, (kind, t) in enumerate(STK):
                        if kind == "v":
                            dve.wait_ge(s["stk_mm"], i * 9 + n + 1)
                            ve.tensor_copy(vx[:, :, :, 0:HD], ps[:, n % 6, :].rearrange(
                                "p (a b c) -> p a b c", a=NT, b=NH)).then_inc(s["stk_r"], 1)
                            continue
                        m = SPLITS.index(n)
                        dve.wait_ge(s["stk_t"], i * 8 + m + 1)
                        if kind == "k":
                            ve.scalar_tensor_tensor(out=kst[:, t, :], in0=ps[:, n % 6, :],
                                                    scalar=cst[:, C_ONE2:C_ONE2 + 1],
                                                    in1=hit[:, m % 2, :].bitcast(F32), op0=ALU.add, op1=ALU.subtract)\
                                .then_inc(s["stk_r"], 1)
                        else:
                            ve.tensor_tensor(qst[:, t, :], ps[:, n % 6, :], hit[:, m % 2, :].bitcast(F32),
                                             ALU.subtract).then_inc(s["stk_r"], 1)

                    for ev in each_step(l):
                        for kind, n in ev:
                            if kind == "s":
                                t, q, jp = n // 8, n % 8 // 2, n % 2
                                dve.wait_ge(s["s_mm"], i * 32 + n + 1)
                                ve.tensor_reduce(mx[:, t, q, 2 * jp:2 * jp + 2], ps[:, 0:2, :], AX.X, ALU.max)\
                                    .then_inc(s["s_red"], 1)
                                if n % 8 == 7:
                                    dve.wait_ge(s["s_red"], i * 32 + n + 1)
                                    cols = shc[:, :, :].rearrange("p a (j r) -> p a j r", r=32)[:, :, :, 0:SHIFT_ROWS]
                                    bg = bet[:, HG * t:HG * t + HG].unsqueeze(1).to_broadcast([P, NT, HG])
                                    if l == 0:
                                        ve.tensor_tensor(mxb[:, :, :], mx[:, t, :, :], bg, ALU.add)\
                                            .then_inc(s["sh_b"], 1)
                                    else:
                                        ve.tensor_scalar(mxb[:, :, :], mx[:, t, :, :], 1.0, None, ALU.add)\
                                            .then_inc(s["sh_b"], 1)
                                    dve.wait_ge(s["sh_b"], i * 4 + t + 1)
                                    if t >= 1:
                                        dve.wait_ge(s["sh_mm"], i * 4 + t)
                                    for r in range(SHIFT_ROWS):
                                        if l == 0:
                                            last = ve.tensor_tensor(cols[:, :, :, r], bg, mxb[:, :, :], ALU.subtract)
                                        else:
                                            last = ve.tensor_scalar(cols[:, :, :, r], mxb[:, :, :], -1.0, None,
                                                                    ALU.mult)
                                    last.then_inc(s["sh_c"], 1)
                            elif kind == "shift":
                                dve.wait_ge(s["sh_t"], i * 4 + n + 1)
                                if n >= 1:
                                    dve.wait_ge(s["sh_q"], i * 4 + n)
                                ve.tensor_tensor(shr[:, :], ps[:, B_MISC, :], sht[:, :].bitcast(F32), ALU.subtract)\
                                    .then_inc(s["sh_r"], 1)
                            elif kind == "st" and l == 1:
                                dve.wait_ge(s["sq_p"], i * 32 + n + 1)
                                v = pr[:, n // 2 % P_SLOTS, 2 * (n % 2):2 * (n % 2) + 2, :]
                                ve.scalar_tensor_tensor(out=v, in0=v, scalar=3.0,
                                                        in1=ps[:, 2 + 2 * (n % 2):4 + 2 * (n % 2), :],
                                                        op0=ALU.add, op1=ALU.mult).then_inc(s["y_p"], 1)
                            elif kind == "out":
                                dve.wait_ge(s["o_tr"], i * 4 + n + 1)
                                v = ps[:, B_MISC, :].rearrange("p (a j r) -> p a j r", a=NT, r=32)
                                ve.reciprocal(orec[:, :, :], v[:, :, :, HD]).then_inc(s["o_rc"], 1)
                                dve.wait_ge(s["o_rc"], i * 4 + n + 1)
                                ve.tensor_tensor(
                                    a[:, :, n * HG * HD:(n + 1) * HG * HD].rearrange("p a (j d) -> p a j d", d=HD),
                                    v[:, :, :, 0:HD], orec[:, :, :].unsqueeze(3).to_broadcast([P, NT, HG, HD]),
                                    ALU.mult).then_inc(s["o_n"], 1)
                    dve.wait_ge(s["proj"], i + 1)
                    g0 = l * M_PER + M_GA
                    ve.scalar_tensor_tensor(out=x[:, :], in0=ps[:, 0, :], scalar=mb[:, g0:g0 + 1], in1=x[:, :],
                                            op0=ALU.mult, op1=ALU.add).then_inc(s["xa1"], 1)
                    dve.wait_ge(s["xa1"], i + 1)
                    ve.tensor_scalar(x[:, :], x[:, :], mb[:, g0 + 1:g0 + 2], None, ALU.add).then_inc(s["xa2"], 1)

                    norm(1)
                    dve.wait_ge(s["hr"], i * 2 + 2)
                    dve.wait_ge(s["hhir"], i + 1)
                    ve.tensor_tensor(hlo, h[:, :], hhi.bitcast(F32), ALU.subtract).then_inc(s["hlor"], 1)

                    rc = [0]

                    def rt(ins, at=None):
                        rc[0] += 1
                        ins.then_inc(s["rt_d"], 1)
                        dve.wait_ge(s["rt_d"], i * RT_N[l] + rc[0])
                        assert at is None or at == rc[0], rc[0]

                    def bc(t):
                        return t.unsqueeze(2).to_broadcast([P, NT, E])

                    dve.wait_ge(s["rt_mm"], i + 1)
                    lgp = ps[:, 0, 0:NT * E].rearrange("p (a b) -> p a b", a=NT)
                    le, ee, re, me = lg[:, :, 0:E], ex[:, :, 0:E], rsc[:, :, 0:E], msk[:, :, 0:E]
                    if l == 0:
                        rt(ve.tensor_copy(le, lgp))
                    else:
                        rt(ve.tensor_tensor(le, lgp, rb[:, :].unsqueeze(1).to_broadcast([P, NT, E]), ALU.add))
                    rt(ve.tensor_reduce(r1[:, :], le, AX.X, ALU.max))
                    rt(ve.tensor_tensor(le, le, bc(r1[:, :]), ALU.subtract), RT_EXP)
                    dve.wait_ge(s["rt_e"], i * (2 - l) + 1)
                    rt(ve.tensor_reduce(r1[:, :], ee, AX.X, ALU.add))
                    rt(ve.reciprocal(r2[:, :], r1[:, :]))
                    rt(ve.tensor_tensor(re, ee, bc(r2[:, :]), ALU.mult))
                    dve.nop(nofuse=True)
                    for q in range(NT):
                        last = ve.max(top[:, q, :], rsc[:, q, 0:E])
                    rt(last)
                    dve.nop(nofuse=True)
                    for q in range(NT):
                        last = ve.max_index(topi[:, q, :], top[:, q, :], rsc[:, q, 0:E])
                    rt(last)
                    rt(ve.tensor_copy(topf[:, :, :], topi[:, :, :]))
                    K = TOPK[l]
                    iota = cst[:, C_IOTA:C_IOTA + E]
                    for q in range(NT):
                        last = ve.tensor_tensor(eq[:, q, 0:E, 0:K], iota.unsqueeze(2).to_broadcast([P, E, K]),
                                                topf[:, q, 0:K].unsqueeze(1).to_broadcast([P, E, K]), ALU.is_equal)
                    rt(last)
                    rt(ve.tensor_reduce(me, eq[:, :, 0:E, 0:K], AX.X, ALU.add))
                    if l == 0:
                        rt(ve.tensor_tensor(le, re, bc(top[:, :, 0]), ALU.subtract), RT_EXP2)
                        dve.wait_ge(s["rt_e"], i * 2 + 2)
                        rt(ve.tensor_tensor(re, ee, me, ALU.mult))
                        rt(ve.tensor_reduce(r1[:, :], re, AX.X, ALU.add))
                    else:
                        rt(ve.tensor_tensor(re, re, me, ALU.mult))
                        rt(ve.tensor_reduce(r1[:, :], re, AX.X, ALU.add))
                        rt(ve.tensor_scalar(r1[:, :], r1[:, :], 1e-12, None, ALU.max))
                    rt(ve.reciprocal(r2[:, :], r1[:, :]))
                    assert rc[0] == RT_N[l], (l, rc[0])
                    for r in range(2):
                        last = ve.tensor_tensor(wd[:, :, 32 * r:32 * r + E], re, bc(r2[:, :]), ALU.mult)
                    last.then_inc(s["w_c"], 1)
                    dve.wait_ge(s["w_t"], i + 1)
                    ve.tensor_tensor(wst, ps[:, B_MISC, :], wt.bitcast(F32), ALU.subtract)\
                        .then_inc(s["w_r"], 1)
                    for c in range(NCH):
                        e = c // PER_EXPERT[l]
                        dve.wait_ge(s["sil_r"], i * NCH + c + 1)
                        src = sil[:, c % 2, :]
                        if c < EC:
                            dve.wait_ge(s["wb"], i * E + e + 1)
                            ve.tensor_tensor(swt[:, c % 2, :], src, ps[:, 4 + e % 2, :], ALU.mult)\
                                .then_inc(s["t_r"], 1)
                            dve.wait_ge(s["t_r"], i * EC + c + 1)
                            src = swt[:, c % 2, :]
                        dve.wait_ge(s["u_mm"], i * NCH + c + 1)
                        if c >= 2:
                            dve.wait_ge(s["dn"], i * NCH + c - 1)
                        ve.tensor_tensor(hid[:, c % 2, :], src, ps[:, 2 + c % 2, :], ALU.mult).then_inc(s["h_r"], 1)
                    dve.wait_ge(s["dn"], i * NCH + NCH)
                    g0 = l * M_PER + M_GB
                    ve.scalar_tensor_tensor(out=x[:, :], in0=ps[:, B_PV, :], scalar=mb[:, g0:g0 + 1], in1=x[:, :],
                                            op0=ALU.mult, op1=ALU.add).then_inc(s["xf"], 1)


RT_N = [15, 15]
RT_EXP = 3
RT_EXP2 = 12
PRE = {"hm": 25, "kd": 27, "qk": 28, "ax": 29, "psi": 30, "sq": 32, "lng": 34, "term": 37, "all": 40}


def layouts(np, d):
    z = {}
    x = d["L0_attn_x"]
    z["xT"] = x.transpose(0, 2, 1)

    def stack(w):
        s = np.zeros((P, NG, HG, 32), np.float32)
        v = w.reshape(P, NG, HG, HD)
        for r in range(3):
            s[:, :, :, COPY0 + HD * r:COPY0 + HD * (r + 1)] = v
        return s.reshape(P, 512)

    qkv = [d["L0_attn_Wqkv"], d["L1_attn_w_qkv"].T]
    wo = [d["L0_attn_Wproj"], d["L1_attn_w_out"].T]
    z["attw"] = np.stack([np.concatenate([stack(qkv[l][:, 0:P]), stack(qkv[l][:, P:2 * P]), qkv[l][:, 2 * P:], wo[l]],
                                         axis=1) for l in range(2)])
    z["alpha"] = np.repeat(d["L0_attn_alpha"].reshape(NG * HG, 1), 32, axis=1).reshape(512)
    z["beta"] = d["L0_attn_beta"]
    z["modw"] = np.stack([d["L0_wmod"], d["L1_wmod"]])
    c = np.zeros((P, C_COLS), np.float32)
    p = np.arange(P)
    c[:, C_ID:C_ID + P] = np.eye(P)
    c[:, C_ONES:C_ONES + P] = 1.0 / P
    row = p % 32
    c[:, C_LOQ] = (row >= COPY0 + 2 * HD)
    c[:, C_LOK] = (row >= COPY0 + HD) & (row < COPY0 + 2 * HD)
    c[:, C_LOS] = row == 1
    c[:, C_LOW] = (p >= 32) & (p < 64)
    c[:, C_ONE2] = row < SHIFT_ROWS
    c[:, C_ONE2 + 1] = EPS
    c[:, C_ONE2 + 2] = 1.0 / 3.0
    c[p, C_HEAD + p // HD] = 1.0
    c[p, C_RQ + p % HD] = 1.0
    c[p, C_RK + HD + p % HD] = 1.0
    for q in range(P):
        c[q % HD, C_RT + q] = 1.0
    for g in range(4):
        c[16 * g:16 * g + 16, C_BM + 16 * g:C_BM + 16 * g + 16] = 1.0 / 16
    c[:, C_IOTA:C_IOTA + 32] = np.arange(32)
    q = np.arange(64)
    c[q, C_SEL + q % 32] = 1.0
    z["consts"] = c
    k = np.zeros((P, K_COLS), np.float32)
    k[:, K_WQ:K_WQ + P] = qkv[0][:, 0:P]
    k[:, K_WK:K_WK + P] = qkv[0][:, P:2 * P]
    T = 4
    k[0:16, K_P1:K_P1 + 32] = d["L0_attn_Wphi1"].transpose(1, 0, 2).reshape(16, 32)
    k[0:16, K_A:K_A + 64] = d["L0_attn_A"].transpose(1, 0, 2).reshape(16, 64)
    for t in range(T):
        k[8 * t:8 * t + 8, K_P2 + 2 * t:K_P2 + 2 * t + 2] = d["L0_attn_Wphi2"][t]
        k[16 * t:16 * t + 16, K_PS1 + 16 * t:K_PS1 + 16 * t + 16] = d["L0_attn_Wpsi1"][t]
        k[16 * t:16 * t + 16, K_PS2 + 2 * t:K_PS2 + 2 * t + 2] = d["L0_attn_Wpsi2"][t]
    k[0:32, K_BP1] = d["L0_attn_bphi1"].reshape(32)
    k[0:8, K_BP2] = d["L0_attn_bphi2"].reshape(8)
    k[0:64, K_BS1] = d["L0_attn_bpsi1"].reshape(64)
    k[0:64, K_G] = d["L0_attn_ln_g"].reshape(64)
    k[0:64, K_B] = d["L0_attn_ln_b"].reshape(64)
    k[0:8, K_BS2] = d["L0_attn_bpsi2"].reshape(8)
    k[0:8, K_MIX] = np.repeat(d["L0_attn_mixing"], 2)
    k[0:8, K_TEMP] = d["L0_attn_temp_scale"]
    k[:, K_GAMMA] = np.repeat(d["L0_attn_gamma"], HD)
    k[:, K_BO] = d["L0_attn_bproj"]
    k[:, K_BO + 1] = d["L1_attn_b_out"]
    nb = x.shape[0]
    k[:, K_C:K_C + nb] = d["L0_c"].T
    k[:, K_C + nb:K_C + 2 * nb] = d["L1_c"].T
    z["kaw"] = k
    z["ffg"] = d["L0_ffn_kernel_gating_EDF"].transpose(1, 0, 2).reshape(P, -1)
    z["ffu"] = d["L0_ffn_kernel_up_EDF"].transpose(1, 0, 2).reshape(P, -1)
    z["ffd0"] = d["L0_ffn_kernel_down_EFD"].reshape(CHUNKS[0], P, P).transpose(1, 0, 2).reshape(P, -1)
    z["ffg1"] = np.concatenate([d["L1_ffn_gate_w"].transpose(2, 0, 1).reshape(P, -1), d["L1_ffn_sgate_w"].T], axis=1)
    z["ffu1"] = np.concatenate([d["L1_ffn_up_w"].transpose(2, 0, 1).reshape(P, -1), d["L1_ffn_sup_w"].T], axis=1)
    z["ffd1"] = np.concatenate([d["L1_ffn_down_w"].transpose(2, 0, 1).reshape(P, -1),
                                d["L1_ffn_sdown_w"].reshape(P, SHARED[1], P).transpose(2, 1, 0).reshape(P, -1)], axis=1)
    z["router0"] = d["L0_ffn_router_kernel_DE"]
    z["router1"] = d["L1_ffn_router_w"].T
    z["rbias"] = d["L1_ffn_router_bias"]
    return z


def kernel(**inputs):
    import numpy as _np
    import concourse.bacc as _bacc
    from concourse import mybir as _mybir
    from concourse.bass_utils import run_bass_kernel_spmd as _run

    nc = _bacc.Bacc("TRN2", target_bir_lowering=False, num_devices=1)
    z = layouts(_np, {k: _np.asarray(v) for k, v in inputs.items()})
    arrays, args = {}, {}
    for name, v in z.items():
        v = _np.ascontiguousarray(v)
        arrays[f"in_{name}"] = v
        args[name] = nc.dram_tensor(f"in_{name}", v.shape, _mybir.dt.from_np(v.dtype), kind="ExternalInput").ap()
    out = nc.dram_tensor("out_T", z["xT"].shape, _mybir.dt.float32, kind="ExternalOutput").ap()
    bass_adaln_two_layers_kernel(nc, outT=out, **args)
    r = _run(nc, [arrays], core_ids=[0])
    return r.results[0]["out_T"].transpose(0, 2, 1)
```

```python
from contextlib import ExitStack

import concourse.bass as bass
from concourse import mybir

F32 = mybir.dt.float32
F32R = mybir.dt.float32r
U32 = mybir.dt.uint32
ALU = mybir.AluOpType
ACT = mybir.ActivationFunctionType
AX = mybir.AxisListType

P = 128
NH = 16
HD = P // NH
HG = 4
NG = NH // HG
TOK = 512
NT = TOK // P
TEMPERATURE = 0.72
EPS = 1e-5
EXPERTS = [8, 32]
PER_EXPERT = [2, 1]
SHARED = [0, 4]
TOPK = [2, 4]
CHUNKS = [EXPERTS[l] * PER_EXPERT[l] + SHARED[l] for l in range(2)]
SHIFT_ROWS = 2
COPY0 = 8
M_SA, M_CA, M_GA, M_GAB, M_SB, M_CB, M_GB, M_PER = 0, 1, 2, 3, 4, 5, 6, 7
M_VAL = 14
M_COLS = 16

GT = NT * HG
NS = NG * GT
TLAG = [22, 24]
PV_LAG = [3, 4]
AFTER = [1, 1]
RECIP_LAG = [0, 0]
P_TILES = 8
KZ_SLOTS = 3
Q_SLOT = [0, 1, 2, 0]
CHUNK_STEP = [4, 2]
CHUNK0 = [20, 17]
LAGS = [{"spread": 0,
         "gate": 0,
         "sigmoid_ln": 0,
         "sigmoid_exp": 1,
         "silu": 2,
         "weigh": 2,
         "up": 3,
         "hidden": 4,
         "down": 6},
        {"spread": 0,
         "gate": 0,
         "sigmoid_ln": 0,
         "sigmoid_exp": 1,
         "silu": 1,
         "weigh": 1,
         "up": 2,
         "hidden": 3,
         "down": 4}]
HEAD = [{"mean1": 0,
         "centre1": 1,
         "var1": 4,
         "rstd1": 5,
         "norm1": 6,
         "h_hi": 7,
         "h_lo": 8,
         "route_mm": 10,
         "route1": 11,
         "route_exp": 12,
         "route2": 12,
         "route3": 13,
         "route4": 14,
         "route_exp2": 15,
         "route5": 15,
         "w_tr": 16,
         "w_hi": 17},
        {"mean1": 0,
         "centre1": 1,
         "var1": 4,
         "rstd1": 5,
         "norm1": 6,
         "h_hi": 7,
         "h_lo": 8,
         "route_mm": 10,
         "route1": 11,
         "route_exp": 12,
         "route2": 12,
         "route3": 13,
         "route4": 13,
         "route_exp2": 14,
         "route5": 14,
         "w_tr": 15,
         "w_hi": 16}]
NEXT = [{"mean0": 72, "centre0": 73, "var0": 76, "rstd0": 77, "norm0": 79},
        {"mean0": 68, "centre0": 69, "var0": 72, "rstd0": 73, "norm0": 75}]
ORDER = [["load_attention", "load_next", "k_hi", "q_hi", "shift_hi", "sums", "a_copy", "w_hi", "cubic",
          "score", "turned", "sigmoid_exp", "recip", "pv", "split", "hidden", "silu", "weigh", "gate",
          "recip_exp", "sigmoid_ln", "up", "down", "k_lo", "q_lo", "shift_lo", "heads", "v_copy", "centre0",
          "centre1", "rstd0", "norm0", "rstd1", "norm1", "h_hi", "h_lo", "route1", "route_exp", "route2",
          "route3", "route4", "route_exp2", "route5", "result", "add", "spread", "k_mm", "q_mm", "v_mm",
          "shift_tr", "sums_tr", "a_tr", "proj", "mean0", "var0", "mean1", "var1", "route_mm", "w_tr"],
         ["load_attention", "load_next", "k_hi", "q_hi", "shift_hi", "sums", "a_copy", "w_hi", "cubic",
          "score", "turned", "sigmoid_exp", "recip", "pv", "split", "hidden", "silu", "weigh", "gate",
          "recip_exp", "sigmoid_ln", "up", "down", "k_lo", "q_lo", "shift_lo", "heads", "v_copy", "centre0",
          "centre1", "rstd0", "norm0", "rstd1", "norm1", "h_hi", "h_lo", "route1", "route_exp", "route2",
          "route3", "route4", "route_exp2", "route5", "result", "add", "spread", "k_mm", "q_mm", "v_mm",
          "shift_tr", "sums_tr", "a_tr", "proj", "mean0", "var0", "mean1", "var1", "route_mm", "w_tr"]]
X_KINDS = ("mean1", "centre1", "var1", "rstd1", "norm1", "h_hi", "h_lo", "route_mm", "route1", "route2", "route3",
           "route4", "route5", "route_exp", "route_exp2", "w_tr", "w_hi", "spread", "gate", "sigmoid_ln", "sigmoid_exp", "silu", "weigh", "up", "hidden",
           "down", "result")

C_ID, C_ONES = 0, 128
C_LOQ, C_LOK, C_LOS, C_LOW, C_ONE2 = 256, 257, 258, 259, 260
C_HEAD = 264
C_RQ, C_RK = 280, 296
C_RT = 312
C_BM = 440
C_IOTA = 504
C_SEL = 536
C_COLS = 568
K_WQ, K_WK, K_P1, K_P2, K_A, K_PS1, K_PS2 = 0, 128, 256, 288, 296, 360, 424
K_BP1, K_BP2, K_BS1, K_G, K_B, K_BS2, K_MIX, K_TEMP, K_GAMMA = 432, 433, 434, 435, 436, 437, 438, 439, 440
K_BO = 441
K_C = 443
K_COLS = 459
A_Q, A_K, A_V, A_O, A_COLS = 0, 512, 1024, 1152, 1280


def bass_adaln_two_layers_kernel(nc, xT, attw, alpha, beta, modw, consts, kaw, ffg, ffu, ffd0, ffg1, ffu1, ffd1,
                                 router0, router1, rbias, outT):
    NB = xT.shape[0]
    ctx = ExitStack()
    with ctx:
        def sb(name, shape, dt=F32):
            return ctx.enter_context(nc.sbuf_tensor(name, shape, dt))

        def sem(name):
            return ctx.enter_context(nc.semaphore(name))

        w_rows = nc.dram_tensor("w_rows", [2, NB, max(EXPERTS), TOK], F32, kind="Internal").ap()
        x1T = nc.dram_tensor("x1T", [NB, P, TOK], F32, kind="Internal").ap()

        ps = ctx.enter_context(nc.psum_tensor("ps", [P, 8, TOK], F32))
        B_S = [[0], [0]]
        B_FIRST = [0, 1, 2, 3, 6]
        B_ST, B_PV, B_MISC, B_ACC = 2, 4, 5, 7
        B_G, B_U = [1, 1], [6, 6]

        cst = sb("cst", [P, C_COLS])
        ident = cst[:, C_ID:C_ID + P]
        ones = cst[:, C_ONES:C_ONES + P]
        aw = sb("aw", [P, A_COLS])
        bet = sb("bet", [P, NH])
        rw = [sb(f"rw{l}", [P, EXPERTS[l]]) for l in range(2)]
        rb = sb("rb", [P, EXPERTS[1]])
        MC = max(CHUNKS)
        whi = sb("whi", [P, 2, MC, P], F32R)
        wlo = sb("wlo", [P, 2, MC, P], F32R)
        wdn = sb("wdn", [P, MC, P])
        modb = sb("modb", [P, NB, M_COLS])
        mbn = sb("mbn", [P, 2])
        mba = sb("mba", [P, M_COLS])
        mbx = sb("mbx", [P, M_COLS])
        sc = sb("sc", [P, 2, NB])
        mabs = sb("mabs", [P, 2, 2, NB])
        msgn = sb("msgn", [P, 2, 2, NB])
        hsum = sb("hsum", [P, NB])
        kd = sb("kd", [P, 2, NB, NH])

        xn = sb("xn", [P, TOK])
        xa = sb("xa", [P, TOK])
        xe = sb("xe", [P, TOK])
        xc = sb("xc", [P, TOK])
        sq = sb("sq", [P, TOK])
        h = sb("h", [P, TOK])
        hhi = sb("hhi", [P, TOK], F32R)
        hlo = sb("hlo", [P, TOK], F32R)
        wt = sb("wt", [32, TOK])
        wbr = sb("wbr", [P, 2, TOK])
        ebuf = sb("ebuf", [P, 4, TOK])
        sil, hid = ebuf[:, 0:2, :], ebuf[:, 2:4, :]
        h1 = ebuf[:, 3, :]
        pr = sb("pr", [P, P_TILES, TOK])
        stage = pr[:, :, :].rearrange("p a c -> p (a c)")
        alph = stage[:, 3 * TOK:4 * TOK]
        kw = xa[:, 0:K_COLS]
        kt = stage[:, 4 * TOK:4 * TOK + 14 * P].rearrange("p (a b) -> p a b", b=P)
        qst = sb("qst", [P, 3, TOK], F32R)
        kst = sb("kst", [P, 2, TOK])
        hit = sb("hit", [P, 2, TOK], F32R)
        kz = sb("kz", [P, KZ_SLOTS, HG, TOK], F32R)
        vx = sb("vx", [P, NT, NH, 32])
        mx = sb("mx", [P, NG, NT, HG])
        mxb = sb("mxb", [P, NT, HG])
        shc = sb("shc", [P, NT, P])
        shr = sb("shr", [P, TOK], F32R)
        o = sb("o", [P, TOK])
        orec = sb("orec", [P, NT, HG])
        a = sb("a", [P, NT, P])
        lg = sb("lg", [P, NT, 32])
        ex = sb("ex", [P, NT, 32])
        rsc = sb("rsc", [P, NT, 32])
        r1 = sb("r1", [P, NT])
        r2 = sb("r2", [P, NT])
        top = sb("top", [P, NT, 8])
        topi = sb("topi", [P, NT, 8], U32)
        topf = sb("topf", [P, NT, 8])
        eq = sb("eq", [P, NT, 32, 4])
        msk = sb("msk", [P, NT, 32])
        wd = sb("wd", [P, NT, P])

        c_in = sem("c_in")
        w_in = sem("w_in")
        g_in = sem("g_in")
        px_in = sem("px_in")
        zero_p = sem("zero_p")
        ones_set = sem("ones_set")
        pdve = sem("pdve")
        pact = sem("pact")
        ppe = sem("ppe")
        lmean = sem("lmean")
        lcent = sem("lcent")
        lsq = sem("lsq")
        lvar = sem("lvar")
        llog = sem("llog")
        lrs = sem("lrs")
        lnorm = sem("lnorm")
        lh = sem("lh")
        lsum = sem("lsum")
        scaled = sem("scaled")
        N_CONST = 9

        block = ctx.enter_context(nc.Block())

        PE_MOD, PE_QM, PE_QK, PE_P1, PE_AX, PE_PS, PE_MU, PE_VAR, PE_PH, PE_PSI, PE_KA = range(1, 12)
        ACT_SILU, ACT_ABS, ACT_PH1, ACT_VAR, ACT_RS, ACT_GELU = range(1, 7)

        D_HM, D_KD, D_QK, D_AX, D_PS, D_SQ, D_LNG, D_TERM, D_ALL = (
            PRE["hm"], PRE["kd"], PRE["qk"], PRE["ax"], PRE["psi"], PRE["sq"], PRE["lng"], PRE["term"], PRE["all"])

        def sems(l):
            names = ("xn_in xa_in x_out mbnr mbar mbxr mom0 cent0 sqd0 logv0 rstd0 norm0 hr0 "
                     "mom1 cent1 sqd1 logv1 rstd1 norm1 hr1 stk_mm stk_t stk_r kzr s_mm s_red "
                     "sh_b sh_c sh_mm sh_t sh_r sh_q st_mm p_r pv o_c o_tr o_rc o_n a_tr a_ev proj xa1 xa2 "
                     "hhir hlor rt_mm rt_d rt_e w_c w_tr w_r w_out g_mm u_mm e_r l_r sil_r a_r t_r h_r dn xf").split()
            if l == 1:
                names += ["sq_p", "y_p", "ln_p"]
            return {n: sem(f"{n}{l}") for n in names}

        S = [sems(0), sems(1)]
        wsp = sem("wsp")
        wspd = sem("wspd")
        wb_in = [sem(f"wb_in{n}") for n in range(2)]
        wstg = [sem(f"wstg{n}") for n in range(4)]

        ffw = [(ffg, ffu, ffd0), (ffg1, ffu1, ffd1)]
        PIECE = 4

        def pieces(l):
            return [(m, c0, min(PIECE, CHUNKS[l] - c0)) for m in range(2) for c0 in range(0, CHUNKS[l], PIECE)]

        def split_count(l, n):
            return l * len(pieces(0)) + n

        def staged(n):
            return ebuf[:, n % 4, :]

        srcx = [xT, x1T]
        dstx = [x1T, outT]

        STK = [("k", 0), ("q", 0), ("v", 0)] + [(w, t) for t in range(1, NG) for w in "kq"]
        STK_K = [STK.index(("k", t)) for t in range(NG)]
        STK_Q = [STK.index(("q", t)) for t in range(NG)]
        SPLITS = [n for n, (w, _) in enumerate(STK) if w != "v"]

        def at(b, per, k):
            reg, off = b
            return off * per + k if reg is None else reg * per + (off * per + k)

        def index(b):
            reg, off = b
            return off if reg is None else reg + off

        def score_bank(l, n):
            return B_FIRST[n % len(B_FIRST)] if n < GT else B_S[l][n % len(B_S[l])]

        def score_before(l, n):
            bank = score_bank(l, n)
            m = n - 1
            while m >= 0 and score_bank(l, m) != bank:
                m -= 1
            return m if m >= 0 else -1

        def is_batch(b, k):
            return b[0] is None and b[1] == k

        def wait(eng, semaphore, value):
            if not isinstance(value, int) or value > 0:
                eng.wait_ge(semaphore, value)

        def stacked(t, w, slot):
            return [(slot, w + "_mm", t), (slot + 1, w + "_hi", t), (slot + 1, w + "_lo", t)]

        def slots(l, attention, experts, following, weights):
            EC, NCH, STEP = EXPERTS[l] * PER_EXPERT[l], CHUNKS[l], CHUNK_STEP[l]
            pv0 = TLAG[l] + PV_LAG[l] + HG - 1
            end = AFTER[l] + pv0 + 4 * (NG * NT - 1)
            once = []
            if attention:
                once += [(0, "load_attention", 0)]
                for t in range(NG):
                    if t >= 1:
                        once += stacked(t, "k", GT * t - 10) + stacked(t, "q", GT * t - 8)
                    once += [(GT * t + 18, "shift_tr", t), (GT * t + 19, "shift_hi", t), (GT * t + 19, "shift_lo", t)]
                    s = pv0 + GT * t + 4 * (NT - 1) + AFTER[l]
                    s2 = s + (s + 1) % 2 + 1
                    once += [(s, "sums", t), (s2, "sums_tr", t), (s2 + 1, "heads", t)]
                e = end + end % 2 + 4
                once += [(e, "a_tr", 0), (e + 1, "a_copy", 0), (e + 2, "proj", 0), (e + 3, "add", 0)]
            if following:
                k0 = TLAG[l] + NS
                once += [(40 if attention or experts else 0, "load_next", 0)]
                once += [(slot, kind, 0) for kind, slot in NEXT[l].items()]
                once += stacked(0, "k", k0) + stacked(0, "q", k0 + 2) + [(end + end % 2 + 8, "v_mm", 0), (end + end % 2 + 9, "v_copy", 0)]
            if experts:
                once += [(slot, kind, 0) for kind, slot in HEAD[l].items()]
                once += [
                         (CHUNK0[l] + STEP * (NCH - 1) + LAGS[l]["down"] + 2, "result", 0)]
                for c in range(NCH):
                    for kind, lag in LAGS[l].items():
                        if kind == "spread":
                            if c < EC and c % PER_EXPERT[l] == 0:
                                once += [(CHUNK0[l] + STEP * c + lag, kind, c // PER_EXPERT[l])]
                        elif kind != "weigh" or c < EC:
                            once += [(CHUNK0[l] + STEP * c + lag, kind, c)]
            if attention:
                for n in range(NS):
                    once += [(n, "score", n), (TLAG[l] + n, "turned", n)]
                    if l == 1:
                        once += [(TLAG[l] + n + 1, "cubic", n)]
                        if n % 2:
                            once += [(TLAG[l] + n + 2, "recip", n // 2), (TLAG[l] + n + 2 + RECIP_LAG[l], "recip_exp", n // 2)]
                for n in range(NG * NT):
                    once += [(pv0 + 4 * n, "pv", n)]
            if weights:
                once += [(3 + 4 * n, "split", n) for n in range(len(pieces(l)))]
            once.sort(key=lambda e: (e[0], ORDER[l].index(e[1]), e[2]))
            for _, kind, n in once:
                yield kind, n

        N_KINDS = ("load_next", "mean0", "centre0", "var0", "rstd0", "norm0")

        def phases(eng, emit, before):
            def phase(l, attention, experts, following, weights=False):
                for kind, n in slots(l, attention, experts, following, weights):
                    first = n == 0 and kind in ("k_mm", "k_hi", "k_lo", "q_mm", "q_hi", "q_lo", "v_mm", "v_copy")
                    if first or kind in N_KINDS:
                        ln, b = following
                    elif kind in X_KINDS:
                        ln, b = l, experts
                    else:
                        ln, b = l, attention
                    emit(ln, kind, n, b)

            phase(0, None, None, (0, (None, 0)))
            for l in range(2):
                phase(l, (None, 0), None, (l, (None, 1)), True)
                before(l, (None, 1))
                with eng.Fori(1, NB - 1) as i:
                    before(l, (i, 0))
                    phase(l, (i, 0), (i, -1), (l, (i, 1)))
                before(l, (None, NB - 1))
                phase(l, (None, NB - 1), (None, NB - 2), None)
                phase(l, None, (None, NB - 1), (1, (None, 0)) if l == 0 else None)

        @block.sync
        def _(sp):
            sp.dma_start(cst[:, :], consts).then_inc(c_in, 16)
            sp.dma_start(kw, kaw).then_inc(c_in, 16)
            for l in range(2):
                sp.dma_start(stage[:, l * 768:(l + 1) * 768], modw[l]).then_inc(c_in, 16)
            sp.dma_start(aw[:, :], attw[0]).then_inc(c_in, 16)
            sp.dma_start(alph, alpha.partition_broadcast(P)).then_inc(c_in, 16)
            sp.dma_start(bet[:, :], beta.partition_broadcast(P)).then_inc(c_in, 16)
            sp.dma_start(rw[0][:, :], router0).then_inc(c_in, 16)
            sp.dma_start(rw[1][:, :], router1).then_inc(c_in, 16)
            sp.dma_start(rb[:, :], rbias.partition_broadcast(P)).then_inc(w_in, 16)
            sp.dma_start(xn[:, :], xT[0, :, :]).then_inc(px_in, 16)
            with sp.Fori(1, NB) as i:
                sp.wait_ge(lcent, i)
                sp.dma_start(xn[:, :], xT[i, :, :]).then_inc(px_in, 16)
            sp.wait_ge(lcent, NB)

            def route(l, b):
                sp.wait_ge(S[l]["w_r"], at(b, 1, 1))
                sp.nop(nofuse=True)
                sp.dma_start(w_rows[l, index(b), 0:EXPERTS[l], :], wt[0:EXPERTS[l], :]).then_inc(S[l]["w_out"], 16)
                sp.wait_ge(S[l]["w_out"], at(b, 16, 16))
                sp.nop(nofuse=True)

            def spread(l, b, e):
                if e >= 2:
                    sp.wait_ge(S[l]["t_r"], at(b, EXPERTS[l] * PER_EXPERT[l], (e - 1) * PER_EXPERT[l]))
                    sp.nop(nofuse=True)
                sp.dma_start(wbr[:, e % 2, :], w_rows[l, index(b), e, :].partition_broadcast(P))                    .then_inc(wb_in[e % 2], 16)

            def load_next(l, b):
                wait(sp, S[l]["cent0"], at(b, 1, 0))
                sp.nop(nofuse=True)
                if l == 1:
                    sp.wait_ge(S[0]["x_out"], at(b, 16, 16))
                    sp.nop(nofuse=True)
                    sp.wait_ge(S[0]["cent0"], NB)
                sp.dma_start(xn[:, :], srcx[l][index(b), :, :]).then_inc(S[l]["xn_in"], 16)

            def load_attention(l, b):
                wait(sp, S[l]["xa1"], at(b, 1, 0))
                sp.nop(nofuse=True)
                if l == 1:
                    sp.wait_ge(S[0]["x_out"], at(b, 16, 16))
                    sp.nop(nofuse=True)
                    sp.wait_ge(S[0]["xa1"], NB)
                sp.dma_start(xa[:, :], srcx[l][index(b), :, :]).then_inc(S[l]["xa_in"], 16)

            def store(l, b):
                sp.wait_ge(S[l]["xf"], at(b, 1, 1))
                sp.nop(nofuse=True)
                sp.dma_start(dstx[l][index(b), :, :], xe[:, :]).then_inc(S[l]["x_out"], 16)

            def emit(l, kind, n, b):
                if kind == "load_next":
                    load_next(l, b)
                elif kind == "load_attention":
                    if l == 0 and is_batch(b, 0):
                        sp.wait_ge(pdve, D_ALL)
                    load_attention(l, b)
                elif kind == "w_hi":
                    route(l, b)
                elif kind == "spread":
                    spread(l, b, n)
                elif kind == "result":
                    store(l, b)
                elif kind == "split":
                    if n == 0:
                        if l == 1:
                            sp.wait_ge(S[0]["dn"], NB * CHUNKS[0])
                            sp.wait_ge(S[0]["h_r"], NB * CHUNKS[0])
                        sp.dma_start(wdn[:, 0:CHUNKS[l], :].rearrange("p a b -> p (a b)"), ffw[l][2])                            .then_inc(g_in, 16)
                    w, c0, k = pieces(l)[n]
                    if n >= 4:
                        sp.wait_ge(wsp, split_count(l, n - 3))
                        sp.wait_ge(wspd, split_count(l, n - 3))
                    sp.dma_start(staged(n), ffw[l][w][:, c0 * P:(c0 + k) * P]).then_inc(wstg[n % 4], 16)
                elif kind == "add" and l == 0 and is_batch(b, NB - 1):
                    sp.wait_ge(S[0]["proj"], NB)
                    sp.dma_start(aw[:, :], attw[1]).then_inc(w_in, 16)

            phases(sp, emit, lambda l, b: None)
            for l in range(2):
                sp.wait_ge(S[l]["x_out"], NB * 16)

        @block.gpsimd
        def _(pool):
            s0 = nc.gpsimd.memset(kz[:, :, :, :].bitcast(F32).rearrange("p a b c -> p (a b c)"), 0.0)
            s0.then_inc(zero_p, 1)
            nc.gpsimd.memset(vx[:, :, :, :], 0.0).then_inc(zero_p, 1)
            pool.wait_ge(zero_p, 2)
            nc.gpsimd.memset(vx[:, :, :, HD:HD + 1], 1.0).then_inc(ones_set, 1)
            nc.gpsimd.memset(shc[:, :, :], 0.0).then_inc(ones_set, 1)
            nc.gpsimd.memset(wd[:, :, :], 0.0).then_inc(ones_set, 1)

            full = [None, 0]
            quad = [None, 0]

            def after(last):
                if last[0] is not None:
                    pool.wait_ge(*last)
                    last[0] = None

            def emit(l, kind, n, b):
                s = S[l]
                if kind == "k_lo":
                    after(full)
                    pool.wait_ge(s["stk_r"], at(b, 9, STK_K[n] + 1))
                    wait(pool, s["st_mm"], at(b, NS, GT if n == KZ_SLOTS else 0))
                    pool.nop(nofuse=True)
                    for j in range(HG):
                        q = slice(32 * j, 32 * j + 32)
                        nc.gpsimd.tensor_copy(kz[q, n % KZ_SLOTS, j, :], kst[q, n % 2, :]).then_inc(s["kzr"], 1)
                    quad[:] = [s["kzr"], at(b, 16, 4 * n + 4)]
                elif kind == "shift_lo":
                    after(quad)
                    pool.wait_ge(s["sh_r"], at(b, 4, n + 1))
                    q = Q_SLOT[n]
                    nc.gpsimd.tensor_tensor(qst[:, q, :], qst[:, q, :].bitcast(F32), shr[:, :].bitcast(F32),
                                            ALU.add).then_inc(s["sh_q"], 1)
                    full[:] = [s["sh_q"], at(b, 4, n + 1)]
                elif kind == "weigh":
                    EC = EXPERTS[l] * PER_EXPERT[l]
                    after(quad)
                    pool.wait_ge(s["a_r"], at(b, CHUNKS[l], n + 1))
                    e = n // PER_EXPERT[l]
                    pool.wait_ge(wb_in[e % 2], at(b, 8 * EXPERTS[l], 8 * NB * EXPERTS[0] * l + 16 * (e // 2) + 16))
                    v = sil[:, n % 2, :]
                    nc.gpsimd.tensor_tensor(v, v, wbr[:, e % 2, :], ALU.mult).then_inc(s["t_r"], 1)
                    full[:] = [s["t_r"], at(b, EC, n + 1)]

            def before(l, b):
                full[0] = None
                quad[:] = [S[l]["kzr"], at(b, 16, 4)]

            phases(pool, emit, before)

        @block.tensor
        def _(pe):
            mm = nc.tensor.matmul
            pe.wait_ge(c_in, 16 * N_CONST)
            pe.wait_ge(pact, ACT_SILU)
            for l in range(2):
                for j in range(6):
                    last = mm(ps[:, 0, (l * 6 + j) * NB:(l * 6 + j + 1) * NB],
                              stage[:, l * 768 + j * P:l * 768 + (j + 1) * P], sc[:, l, :], start=True, stop=True)
            last.then_inc(ppe, 1)

            def moments(i):
                pe.wait_ge(px_in, i * 16 + 16)
                wait(pe, lcent, i)
                mm(ps[:, 6, :], ones, xn[:, :], start=True, stop=True).then_inc(lmean, 1)
                pe.wait_ge(lsq, i + 1)
                wait(pe, llog, i)
                mm(ps[:, 7, :], ones, sq[:, :], start=True, stop=True).then_inc(lvar, 1)

            moments(0)
            with pe.Fori(1, NB) as i:
                moments(i)
            pe.wait_ge(pdve, D_HM)
            mm(ps[:, 1, 0:NB], kw[:, K_WQ:K_WQ + P], hsum[:, :], start=True, stop=True)
            mm(ps[:, 1, NB:2 * NB], kw[:, K_WK:K_WK + P], hsum[:, :], start=True, stop=True).then_inc(ppe, 1)
            pe.wait_ge(pdve, D_KD)
            for n, c in enumerate((C_RQ, C_RK)):
                last = mm(ps[0:16, 2, 0:P], cst[:, c:c + 16], kd[:, n, :, :].rearrange("p a b -> p (a b)"),
                          start=(n == 0), stop=(n == 1))
            last.then_inc(ppe, 1)
            pe.wait_ge(pdve, D_QK)
            mm(ps[0:32, 3, 0:P], kw[0:16, K_P1:K_P1 + 32], kt[0:16, 0, :], start=True, stop=True).then_inc(ppe, 1)
            mm(ps[0:64, 4, 0:P], kw[0:16, K_A:K_A + 64], kt[0:16, 0, :], start=True, stop=True).then_inc(ppe, 1)
            pe.wait_ge(pdve, D_AX)
            mm(ps[0:64, 5, 0:P], kw[0:64, K_PS1:K_PS1 + 64], kt[0:64, 1, :], start=True, stop=True).then_inc(ppe, 1)
            pe.wait_ge(pdve, D_PS)
            mm(ps[0:64, 4, 0:P], cst[0:64, C_BM:C_BM + 64], kt[0:64, 2, :], start=True, stop=True).then_inc(ppe, 1)
            pe.wait_ge(pdve, D_SQ)
            mm(ps[0:64, 5, 0:P], cst[0:64, C_BM:C_BM + 64], kt[0:64, 4, :], start=True, stop=True).then_inc(ppe, 1)
            pe.wait_ge(pact, ACT_PH1)
            mm(ps[0:8, 2, 0:P], kw[0:32, K_P2:K_P2 + 8], kt[0:32, 5, :], start=True, stop=True).then_inc(ppe, 1)
            pe.wait_ge(pact, ACT_GELU)
            mm(ps[0:8, 3, 0:P], kw[0:64, K_PS2:K_PS2 + 8], kt[0:64, 9, :], start=True, stop=True).then_inc(ppe, 1)
            pe.wait_ge(pdve, D_TERM)
            mm(ps[:, 4, 0:P], cst[0:8, C_RT:C_RT + P], kt[0:8, 12, :], start=True, stop=True).then_inc(ppe, 1)
            pe.wait_ge(ones_set, 3)

            misc = [S[0]["cent0"], 0]

            def take(semaphore, value):
                wait(pe, *misc)
                misc[:] = [semaphore, value]

            def emit(l, kind, n, b):
                s = S[l]
                E, NCH = EXPERTS[l], CHUNKS[l]
                EC = E * PER_EXPERT[l]
                m = ps[:, B_MISC, :]
                if kind == "mean0":
                    pe.wait_ge(s["xn_in"], at(b, 16, 16))
                    take(s["cent0"], at(b, 1, 1))
                    mm(m, ones, xn[:, :], start=True, stop=True).then_inc(s["mom0"], 1)
                elif kind == "mean1":
                    pe.wait_ge(s["xa2"], at(b, 1, 1))
                    take(s["cent1"], at(b, 1, 1))
                    mm(m, ones, xe[:, :], start=True, stop=True).then_inc(s["mom1"], 1)
                elif kind in ("var0", "var1"):
                    k = kind[3]
                    pe.wait_ge(s["sqd" + k], at(b, 1, 1))
                    take(s["logv" + k], at(b, 1, 1))
                    mm(m, ones, sq[:, :], start=True, stop=True).then_inc(s["mom" + k], 1)
                elif kind in ("k_mm", "q_mm"):
                    if l == 1 and is_batch(b, 0):
                        pe.wait_ge(scaled, 1)
                    pe.wait_ge(s["hr0"], at(b, 1, 1))
                    take(s["stk_r"], at(b, 9, STK.index((kind[0], n)) + 1))
                    c = (A_K if kind == "k_mm" else A_Q) + n * P
                    mm(m, aw[:, c:c + P], h[:, :], start=True, stop=True).then_inc(s["stk_mm"], 1)
                elif kind == "v_mm":
                    take(s["stk_r"], at(b, 9, STK.index(("v", 0)) + 1))
                    for q in range(NT):
                        last = mm(m[:, q * P:(q + 1) * P], h[:, q * P:(q + 1) * P], aw[:, A_V:A_V + P],
                                  start=True, stop=True)
                    last.then_inc(s["stk_mm"], 1)
                elif kind == "score":
                    t, q, j = n // GT, n % GT // HG, n % HG
                    if n % GT == 0:
                        pe.wait_ge(s["kzr"], at(b, 16, 4 * t + 4))
                        pe.wait_ge(s["stk_r"], at(b, 9, STK_Q[t] + 1))
                    wait(pe, s["s_red"], at(b, NS, score_before(l, n) + 1))
                    if n == 0:
                        wait(pe, s["p_r"] if l == 0 else s["y_p"], at(b, NS, 0))
                    mm(ps[:, score_bank(l, n), :], qst[:, Q_SLOT[t], q * P:(q + 1) * P], kz[:, t % KZ_SLOTS, j, :],
                       start=True, stop=True).then_inc(s["s_mm"], 1)
                elif kind == "shift_tr":
                    pe.wait_ge(s["sh_c"], at(b, 4, n + 1))
                    take(s["sh_r"], at(b, 4, n + 1))
                    for q in range(NT):
                        last = nc.tensor.transpose(m[:, q * P:(q + 1) * P], shc[:, q, :], ident)
                    last.then_inc(s["sh_mm"], 1)
                elif kind == "turned":
                    t, k, j = n // GT, n % GT // HG, n % HG
                    if n % GT == 0:
                        pe.wait_ge(s["sh_q"], at(b, 4, t + 1))
                    wait(pe, s["p_r"] if l == 0 else s["y_p"], at(b, NS, n - 1))
                    mm(ps[:, B_ST + n % 2, :], kz[:, t % KZ_SLOTS, j, k * P:(k + 1) * P], qst[:, Q_SLOT[t], :],
                       start=True, stop=True).then_inc(s["st_mm"], 1)
                elif kind == "pv":
                    t, k = n // NT, n % NT
                    pe.wait_ge(s["p_r"], at(b, NS, 4 * n + 4) if l == 0 else at(b, NS // 2, 2 * n + 2))
                    if k == 0:
                        wait(pe, s["o_c"], at(b, 4, t))
                    if n == 0:
                        pe.wait_ge(s["stk_r"], at(b, 9, STK.index(("v", 0)) + 1))
                    for j in range(HG):
                        last = mm(ps[32 * j:32 * j + 32, B_PV, :], vx[:, k, HG * t + j, :],
                                  pr[:, (4 * n + j) % P_TILES, :], start=(k == 0), stop=(k == NT - 1))
                    last.then_inc(s["pv"], 1)
                elif kind == "sums_tr":
                    pe.wait_ge(s["o_c"], at(b, 4, n + 1))
                    take(s["o_n"], at(b, 4, n + 1))
                    for q in range(NT):
                        last = nc.tensor.transpose(m[:, q * P:(q + 1) * P], o[:, q * P:(q + 1) * P], ident)
                    last.then_inc(s["o_tr"], 1)
                elif kind == "a_tr":
                    pe.wait_ge(s["o_n"], at(b, 4, 4))
                    take(s["a_ev"], at(b, 1, 1))
                    for q in range(NT):
                        last = nc.tensor.transpose(m[:, q * P:(q + 1) * P], a[:, q, :], ident)
                    last.then_inc(s["a_tr"], 1)
                elif kind == "proj":
                    take(s["xa1"], at(b, 1, 1))
                    mm(m, aw[:, A_O:A_O + P], o[:, :], start=True, stop=True).then_inc(s["proj"], 1)
                elif kind == "route_mm":
                    pe.wait_ge(s["hr1"], at(b, 1, 1))
                    take(s["rt_d"], at(b, RT_N[l], 1))
                    for q in range(NT):
                        last = mm(m[:, q * E:(q + 1) * E], h1[:, q * P:(q + 1) * P], rw[l][:, :],
                                  start=True, stop=True)
                    last.then_inc(s["rt_mm"], 1)
                elif kind == "w_tr":
                    pe.wait_ge(s["w_c"], at(b, 1, 1))
                    take(s["w_r"], at(b, 1, 1))
                    for q in range(NT):
                        last = nc.tensor.transpose(m[:, q * P:(q + 1) * P], wd[:, q, :], ident)
                    last.then_inc(s["w_tr"], 1)
                elif kind in ("gate", "up"):
                    g = kind == "gate"
                    if g and n == 0:
                        pe.wait_ge(s["hhir"], at(b, 1, 1))
                        pe.wait_ge(s["hlor"], at(b, 1, 1))
                    if B_G[l] == B_U[l] and not g:
                        pe.wait_ge(s["a_r"], at(b, NCH, n + 1))
                    elif n >= 1:
                        pe.wait_ge(s["a_r" if B_G[l] != B_U[l] and g else "h_r"], at(b, NCH, n))
                    bank = ps[:, B_G[l] if g else B_U[l], :]
                    w = 0 if g else 1
                    mm(bank, wlo[:, w, n, :], hhi[:, :], start=True, stop=False)
                    mm(bank, whi[:, w, n, :], hlo[:, :], start=False, stop=False)
                    mm(bank, whi[:, w, n, :], hhi[:, :], start=False, stop=True).then_inc(s["g_mm" if g else "u_mm"], 1)
                elif kind == "down":
                    pe.wait_ge(s["h_r"], at(b, NCH, n + 1))
                    mm(ps[:, B_ACC, :], wdn[:, n, :], hid[:, n % 2, :], start=(n == 0), stop=(n == NCH - 1))\
                        .then_inc(s["dn"], 1)

            def before(l, b):
                misc[:] = [S[l]["stk_r"], at(b, 9, STK.index(("v", 0)) + 1)]
                if is_batch(b, 1):
                    pe.wait_ge(wsp, split_count(l, len(pieces(l))))
                    pe.wait_ge(wspd, split_count(l, len(pieces(l))))
                    pe.wait_ge(g_in, 16 * (l + 1))

            pe.wait_ge(pdve, D_ALL)
            phases(pe, emit, before)
        @block.scalar
        def _(act):
            act.preload_act_table_set("silu_and_others")
            act.wait_ge(c_in, 16 * N_CONST)
            nc.scalar.activation(sc[:, :, :], kw[:, K_C:K_C + 2 * NB].rearrange("p (a b) -> p a b", a=2),
                                 ACT.Silu).then_inc(pact, 1)
            act.wait_ge(ppe, PE_MOD)
            for g in range(2):
                last = nc.scalar.activation(mabs[:, :, g, :],
                                            ps[:, 0, 0:12 * NB].rearrange("p (a b c) -> p a b c", a=2, b=6)[
                                                :, :, 2 + 3 * g, :], ACT.Abs)
            last.then_inc(pact, 1)
            act.preload_act_table_set("natural_log_exp_and_others")
            with act.Fori(0, NB) as i:
                act.wait_ge(lcent, i + 1)
                nc.scalar.activation(sq[:, :], xc[:, :], ACT.Square).then_inc(lsq, 1)
                act.wait_ge(lvar, i + 1)
                nc.scalar.activation(sq[:, :], ps[:, 7, :], ACT.Ln, bias=cst[:, C_ONE2 + 1:C_ONE2 + 2]).then_inc(llog, 1)
                act.wait_ge(llog, i + 1)
                nc.scalar.activation(sq[:, :], sq[:, :], ACT.Exp, scale=-0.5).then_inc(lrs, 1)
            act.wait_ge(ppe, PE_P1)
            nc.scalar.activation(kt[0:32, 5, :], ps[0:32, 3, 0:P], ACT.Silu,
                                 bias=kw[0:32, K_BP1:K_BP1 + 1]).then_inc(pact, 1)
            act.wait_ge(ppe, PE_VAR)
            nc.scalar.activation(kt[0:64, 6, :], ps[0:64, 5, 0:P], ACT.Ln,
                                 bias=cst[0:64, C_ONE2 + 1:C_ONE2 + 2]).then_inc(pact, 1)
            act.wait_ge(pact, ACT_VAR)
            nc.scalar.activation(kt[0:64, 7, :], kt[0:64, 6, :], ACT.Exp, scale=-0.5).then_inc(pact, 1)
            act.wait_ge(pdve, D_LNG)
            nc.scalar.activation(kt[0:64, 9, :], kt[0:64, 8, :], ACT.Gelu).then_inc(pact, 1)

            def emit(l, kind, n, b):
                s = S[l]
                E, NCH = EXPERTS[l], CHUNKS[l]
                m = ps[:, B_MISC, :]
                if kind in ("centre0", "centre1"):
                    k = kind[6]
                    act.wait_ge(s["cent" + k], at(b, 1, 1))
                    nc.scalar.activation(sq[:, :], xc[:, :], ACT.Square).then_inc(s["sqd" + k], 1)
                elif kind in ("rstd0", "rstd1"):
                    k = kind[4]
                    act.wait_ge(s["mom" + k], at(b, 2, 2))
                    nc.scalar.activation(sq[:, :], m, ACT.Ln, bias=cst[:, C_ONE2 + 1:C_ONE2 + 2])\
                        .then_inc(s["logv" + k], 1)
                    act.wait_ge(s["logv" + k], at(b, 1, 1))
                    nc.scalar.activation(sq[:, :], sq[:, :], ACT.Exp, scale=-0.5).then_inc(s[kind], 1)
                elif kind in ("k_hi", "q_hi"):
                    p = STK.index((kind[0], n))
                    act.wait_ge(s["stk_mm"], at(b, 9, p + 1))
                    lo = cst[:, C_LOK:C_LOK + 1] if kind == "k_hi" else cst[:, C_LOQ:C_LOQ + 1]
                    nc.scalar.activation(hit[:, kind == "q_hi", :], m, ACT.Copy, scale=lo).then_inc(s["stk_t"], 1)
                elif kind == "shift_hi":
                    act.wait_ge(s["sh_mm"], at(b, 4, n + 1))
                    wait(act, s["sh_q"], at(b, 4, n))
                    nc.scalar.activation(shr[:, :], m, ACT.Copy, scale=cst[:, C_LOS:C_LOS + 1]).then_inc(s["sh_t"], 1)
                elif kind == "turned":
                    act.wait_ge(s["st_mm"], at(b, NS, n + 1))
                    if n % HG == 0:
                        wait(act, s["pv"], at(b, 16, n // HG - 1))
                    dst = pr[:, n % P_TILES, :]
                    src = ps[:, B_ST + n % 2, :]
                    if l == 0:
                        nc.scalar.activation(dst, src, ACT.Exp).then_inc(s["p_r"], 1)
                    else:
                        nc.scalar.activation(dst, src, ACT.Square).then_inc(s["sq_p"], 1)
                elif kind == "recip":
                    act.wait_ge(s["y_p"], at(b, NS, 2 * n + 2))
                    v = pr[:, 2 * n % P_TILES:2 * n % P_TILES + 2, :]
                    nc.scalar.activation(v, v, ACT.Ln, scale=-1.0 / 6.0, bias=cst[:, C_ONE2 + 2:C_ONE2 + 3])\
                        .then_inc(s["ln_p"], 1)
                elif kind == "recip_exp":
                    v = pr[:, 2 * n % P_TILES:2 * n % P_TILES + 2, :]
                    act.wait_ge(s["ln_p"], at(b, NS // 2, n + 1))
                    nc.scalar.activation(v, v, ACT.Exp, scale=-1.0).then_inc(s["p_r"], 1)
                elif kind == "sums":
                    act.wait_ge(s["pv"], at(b, 16, NT * n + NT))
                    if n >= 1:
                        act.wait_ge(s["o_tr"], at(b, 4, n))
                    else:
                        wait(act, s["proj"], at(b, 1, 0))
                    nc.scalar.activation(o[:, :], ps[:, B_PV, :], ACT.Copy).then_inc(s["o_c"], 1)
                elif kind == "a_copy":
                    act.wait_ge(s["a_tr"], at(b, 1, 1))
                    if l == 0:
                        act.wait_ge(s["mbar"], at(b, 1, 1))
                        nc.scalar.activation(o[:, :], m, ACT.Copy, scale=mba[:, M_VAL:M_VAL + 1])\
                            .then_inc(s["a_ev"], 1)
                    else:
                        nc.scalar.activation(o[:, :], m, ACT.Copy).then_inc(s["a_ev"], 1)
                elif kind == "split":
                    w, c0, k = pieces(l)[n]
                    act.wait_ge(wstg[n % 4], 16 * (split_count(l, n) // 4) + 16)
                    nc.scalar.activation(whi[:, w, c0:c0 + k, :].rearrange("p a b -> p (a b)"), staged(n),
                                         ACT.Copy).then_inc(wsp, 1)
                elif kind == "h_hi":
                    act.wait_ge(s["norm1"], at(b, 1, 1))
                    act.wait_ge(s["mbxr"], at(b, 1, 1))
                    o0 = l * M_PER + M_SB
                    nc.scalar.activation(hhi[:, :], xc[:, :], ACT.Identity, scale=mbx[:, o0 + 1:o0 + 2],
                                         bias=mbx[:, o0:o0 + 1]).then_inc(s["hhir"], 1)
                elif kind == "route_exp" or (kind == "route_exp2" and l == 0):
                    act.wait_ge(s["rt_d"], at(b, RT_N[l], RT_EXP if kind == "route_exp" else RT_EXP2))
                    nc.scalar.activation(ex[:, :, 0:E], lg[:, :, 0:E], ACT.Exp).then_inc(s["rt_e"], 1)
                elif kind == "w_hi":
                    act.wait_ge(s["w_tr"], at(b, 1, 1))
                    nc.scalar.activation(wt[:, :], m[0:32, :], ACT.Copy).then_inc(s["w_r"], 1)
                elif kind == "gate":
                    act.wait_ge(s["g_mm"], at(b, NCH, n + 1))
                    if n >= 2:
                        act.wait_ge(s["h_r"], at(b, NCH, n - 1))
                    v = sil[:, n % 2, :]
                    nc.scalar.activation(v, ps[:, B_G[l], :], ACT.Exp, scale=-1.0).then_inc(s["e_r"], 1)
                elif kind == "sigmoid_ln":
                    v = sil[:, n % 2, :]
                    act.wait_ge(s["e_r"], at(b, NCH, n + 1))
                    nc.scalar.activation(v, v, ACT.Ln, bias=1.0).then_inc(s["l_r"], 1)
                elif kind == "sigmoid_exp":
                    v = sil[:, n % 2, :]
                    act.wait_ge(s["l_r"], at(b, NCH, n + 1))
                    nc.scalar.activation(v, v, ACT.Exp, scale=-1.0).then_inc(s["sil_r"], 1)

            act.wait_ge(pdve, D_ALL)
            act.preload_act_table_set("natural_log_exp_and_others")
            phases(act, emit, lambda l, b: act.preload_act_table_set("natural_log_exp_and_others"))

        @block.vector
        def _(dve):
            ve = nc.vector
            count = [0]

            def link(ins, name=None):
                count[0] += 1
                ins.then_inc(pdve, 1)
                dve.wait_ge(pdve, count[0])
                if name:
                    assert PRE[name] == count[0], (name, count[0])

            dve.wait_ge(c_in, 16 * N_CONST)
            link(ve.scalar_tensor_tensor(out=aw[:, A_Q:A_Q + 512], in0=aw[:, A_Q:A_Q + 512],
                                         scalar=float(HD) ** -0.5 / TEMPERATURE, in1=alph,
                                         op0=ALU.mult, op1=ALU.mult))
            dve.wait_ge(pact, ACT_ABS)
            for l in range(2):
                mp = ps[:, 0, l * 6 * NB:(l + 1) * 6 * NB].rearrange("p (a b) -> p b a", a=6)
                for g in range(2):
                    o0 = l * M_PER + (M_SA if g == 0 else M_SB)
                    link(ve.tensor_copy(modb[:, :, o0], mp[:, :, 3 * g]))
                    link(ve.tensor_scalar(modb[:, :, o0 + 1], mp[:, :, 3 * g + 1], 1.0, None, ALU.add))
                    link(ve.tensor_scalar(msgn[:, l, g, :], mp[:, :, 3 * g + 2], 0.0, 2.0, ALU.is_ge, ALU.mult))
                    link(ve.tensor_scalar(mabs[:, l, g, :], mabs[:, l, g, :], 0.25, None, ALU.max))
                    link(ve.scalar_tensor_tensor(out=modb[:, :, o0 + 2], in0=msgn[:, l, g, :], scalar=-1.0,
                                                 in1=mabs[:, l, g, :], op0=ALU.add, op1=ALU.mult))
                o0 = l * M_PER
                link(ve.tensor_scalar(modb[:, :, o0 + M_GAB], modb[:, :, o0 + M_GA], kw[:, K_BO + l:K_BO + l + 1],
                                      None, ALU.mult))

            def normed(i):
                dve.wait_ge(lmean, i + 1)
                wait(dve, lh, 2 * i)
                ve.tensor_tensor(xc[:, :], xn[:, :], ps[:, 6, :], ALU.subtract).then_inc(lcent, 1)
                ve.tensor_copy(mba[:, 0:M_VAL], modb[:, bass.ds(i, 1), 0:M_VAL].rearrange("p a b -> p (a b)")).then_inc(lh, 1)
                dve.wait_ge(lcent, i + 1)
                dve.wait_ge(lrs, i + 1)
                ve.tensor_tensor(xc[:, :], xc[:, :], sq[:, :], ALU.mult).then_inc(lnorm, 1)
                dve.wait_ge(lnorm, i + 1)
                dve.wait_ge(lh, 2 * i + 1)
                ve.tensor_scalar(h[:, :], xc[:, :], mba[:, M_CA:M_CA + 1], mba[:, M_SA:M_SA + 1], ALU.mult, ALU.add)\
                    .then_inc(lh, 1)
                dve.wait_ge(lh, 2 * i + 2)
                ve.tensor_reduce(hsum[:, bass.ds(i, 1)], h[:, :], AX.X, ALU.add).then_inc(lsum, 1)

            normed(0)
            with dve.Fori(1, NB) as i:
                normed(i)
            dve.wait_ge(lsum, NB)
            link(ve.tensor_scalar(hsum[:, :], hsum[:, :], 1.0 / TOK, None, ALU.mult), "hm")
            dve.wait_ge(ppe, PE_QM)
            head = cst[:, C_HEAD:C_HEAD + NH].unsqueeze(1).to_broadcast([P, NB, NH])
            for n in range(2):
                link(ve.tensor_tensor(kd[:, n, :, :], head,
                                      ps[:, 1, n * NB:(n + 1) * NB].unsqueeze(2).to_broadcast([P, NB, NH]), ALU.mult),
                     "kd" if n else None)
            dve.wait_ge(ppe, PE_QK)
            link(ve.tensor_copy(kt[0:16, 0, :], ps[0:16, 2, 0:P]), "qk")
            dve.wait_ge(ppe, PE_AX)
            link(ve.tensor_copy(kt[0:64, 1, :], ps[0:64, 4, 0:P]), "ax")
            dve.wait_ge(ppe, PE_PS)
            link(ve.tensor_scalar(kt[0:64, 2, :], ps[0:64, 5, 0:P], kw[0:64, K_BS1:K_BS1 + 1], None, ALU.add), "psi")
            dve.wait_ge(ppe, PE_MU)
            link(ve.tensor_tensor(kt[0:64, 3, :], kt[0:64, 2, :], ps[0:64, 4, 0:P], ALU.subtract))
            link(ve.tensor_tensor(kt[0:64, 4, :], kt[0:64, 3, :], kt[0:64, 3, :], ALU.mult), "sq")
            dve.wait_ge(pact, ACT_RS)
            link(ve.tensor_tensor(kt[0:64, 13, :], kt[0:64, 3, :], kt[0:64, 7, :], ALU.mult))
            link(ve.tensor_scalar(kt[0:64, 8, :], kt[0:64, 13, :], kw[0:64, K_G:K_G + 1], kw[0:64, K_B:K_B + 1],
                                  ALU.mult, ALU.add), "lng")
            dve.wait_ge(ppe, PE_PH)
            link(ve.tensor_scalar(kt[0:8, 10, :], ps[0:8, 2, 0:P], kw[0:8, K_BP2:K_BP2 + 1], None, ALU.add))
            dve.wait_ge(ppe, PE_PSI)
            link(ve.scalar_tensor_tensor(out=kt[0:8, 11, :], in0=ps[0:8, 3, 0:P], scalar=kw[0:8, K_BS2:K_BS2 + 1],
                                         in1=kt[0:8, 10, :], op0=ALU.add, op1=ALU.mult))
            link(ve.tensor_scalar(kt[0:8, 12, :], kt[0:8, 11, :], kw[0:8, K_TEMP:K_TEMP + 1],
                                  kw[0:8, K_MIX:K_MIX + 1], ALU.mult, ALU.mult), "term")
            dve.wait_ge(ppe, PE_KA)
            link(ve.tensor_tensor(kd[:, 0, :, :], head,
                                  ps[:, 4, 0:P].rearrange("p (a b) -> p a b", b=NH), ALU.mult))
            link(ve.tensor_reduce(hsum[:, :], kd[:, 0, :, :], AX.X, ALU.add))
            link(ve.tensor_scalar(modb[:, :, M_VAL], hsum[:, :], 1.0, kw[:, K_GAMMA:K_GAMMA + 1], ALU.add, ALU.mult),
                 "all")
            dve.wait_ge(ones_set, 3)

            def rt(s, l, b, step, ins):
                ins.then_inc(s["rt_d"], 1)
                dve.wait_ge(s["rt_d"], at(b, RT_N[l], step))

            def emit(l, kind, n, b):
                s = S[l]
                E, NCH = EXPERTS[l], CHUNKS[l]
                EC = E * PER_EXPERT[l]
                m = ps[:, B_MISC, :]

                def bc(t):
                    return t.unsqueeze(2).to_broadcast([P, NT, E])

                le, ee, re, me = lg[:, :, 0:E], ex[:, :, 0:E], rsc[:, :, 0:E], msk[:, :, 0:E]
                K = TOPK[l]
                if kind in ("centre0", "centre1"):
                    k = kind[6]
                    src = xn if k == "0" else xe
                    dve.wait_ge(s["mom" + k], at(b, 2, 1))
                    ve.tensor_tensor(xc[:, :], src[:, :], m, ALU.subtract).then_inc(s["cent" + k], 1)
                    if k == "0":
                        if l == 1 and is_batch(b, 0):
                            dve.wait_ge(w_in, 32)
                            ve.tensor_scalar(aw[:, A_Q:A_Q + 512], aw[:, A_Q:A_Q + 512], float(HD) ** -0.5, None,
                                             ALU.mult).then_inc(scaled, 1)
                        o0 = l * M_PER + M_SA
                        ve.tensor_copy(mbn[:, :], modb[:, bass.ds(index(b), 1), o0:o0 + 2].rearrange(
                            "p a b -> p (a b)")).then_inc(s["mbnr"], 1)
                    else:
                        ve.tensor_copy(mbx[:, 0:M_VAL], modb[:, bass.ds(index(b), 1), 0:M_VAL].rearrange("p a b -> p (a b)"))\
                            .then_inc(s["mbxr"], 1)
                elif kind in ("norm0", "norm1"):
                    k = kind[4]
                    dve.wait_ge(s["cent" + k], at(b, 1, 1))
                    dve.wait_ge(s["rstd" + k], at(b, 1, 1))
                    ve.tensor_tensor(xc[:, :], xc[:, :], sq[:, :], ALU.mult).then_inc(s["norm" + k], 1)
                    dve.wait_ge(s["norm" + k], at(b, 1, 1))
                    dve.wait_ge(s["mbnr" if k == "0" else "mbxr"], at(b, 1, 1))
                    o0 = l * M_PER + M_SB
                    dst, f = (h[:, :], mbn[:, 0:2]) if k == "0" else (h1, mbx[:, o0:o0 + 2])
                    ve.tensor_scalar(dst, xc[:, :], f[:, 1:2], f[:, 0:1], ALU.mult, ALU.add).then_inc(s["hr" + k], 1)
                elif kind == "h_lo":
                    dve.wait_ge(s["hr1"], at(b, 1, 1))
                    dve.wait_ge(s["hhir"], at(b, 1, 1))
                    ve.tensor_tensor(hlo[:, :], h1, hhi[:, :].bitcast(F32), ALU.subtract).then_inc(s["hlor"], 1)
                elif kind == "k_lo":
                    p = STK_K[n]
                    dve.wait_ge(s["stk_t"], at(b, 8, SPLITS.index(p) + 1))
                    wait(dve, s["kzr"], at(b, 16, 4 * n - 4))
                    ve.scalar_tensor_tensor(out=kst[:, n % 2, :], in0=m, scalar=cst[:, C_ONE2:C_ONE2 + 1],
                                            in1=hit[:, 0, :].bitcast(F32), op0=ALU.add, op1=ALU.subtract)\
                        .then_inc(s["stk_r"], 1)
                elif kind == "q_lo":
                    p = STK_Q[n]
                    dve.wait_ge(s["stk_t"], at(b, 8, SPLITS.index(p) + 1))
                    wait(dve, s["st_mm"], at(b, NS, GT if n == NG - 1 else 0))
                    ve.tensor_tensor(qst[:, Q_SLOT[n], :], m, hit[:, 1, :].bitcast(F32), ALU.subtract)\
                        .then_inc(s["stk_r"], 1)
                elif kind == "v_copy":
                    dve.wait_ge(s["stk_mm"], at(b, 9, STK.index(("v", 0)) + 1))
                    wait(dve, s["pv"], at(b, 16, 0))
                    ve.tensor_copy(vx[:, :, :, 0:HD], m.rearrange("p (a b c) -> p a b c", a=NT, b=NH))\
                        .then_inc(s["stk_r"], 1)
                elif kind == "score":
                    t, q, j = n // GT, n % GT // HG, n % HG
                    dve.wait_ge(s["s_mm"], at(b, NS, n + 1))
                    ve.tensor_reduce(mx[:, t, q, j:j + 1], ps[:, score_bank(l, n), :], AX.X, ALU.max).then_inc(s["s_red"], 1)
                    if n % GT == GT - 1:
                        dve.wait_ge(s["s_red"], at(b, NS, n + 1))
                        cols = shc[:, :, :].rearrange("p a (j r) -> p a j r", r=32)[:, :, :, 0:SHIFT_ROWS]
                        bg = bet[:, HG * t:HG * t + HG].unsqueeze(1).to_broadcast([P, NT, HG])
                        if l == 0:
                            ve.tensor_tensor(mxb[:, :, :], mx[:, t, :, :], bg, ALU.add).then_inc(s["sh_b"], 1)
                        else:
                            ve.tensor_scalar(mxb[:, :, :], mx[:, t, :, :], 1.0, None, ALU.add).then_inc(s["sh_b"], 1)
                        dve.wait_ge(s["sh_b"], at(b, 4, t + 1))
                        wait(dve, s["sh_mm"], at(b, 4, t))
                        for r in range(SHIFT_ROWS):
                            if l == 0:
                                last = ve.tensor_tensor(cols[:, :, :, r], bg, mxb[:, :, :], ALU.subtract)
                            else:
                                last = ve.tensor_scalar(cols[:, :, :, r], mxb[:, :, :], -1.0, None, ALU.mult)
                        last.then_inc(s["sh_c"], 1)
                elif kind == "shift_lo":
                    dve.wait_ge(s["sh_t"], at(b, 4, n + 1))
                    ve.tensor_tensor(shr[:, :], m, shr[:, :].bitcast(F32), ALU.subtract).then_inc(s["sh_r"], 1)
                elif kind == "cubic":
                    dve.wait_ge(s["sq_p"], at(b, NS, n + 1))
                    v = pr[:, n % P_TILES, :]
                    ve.scalar_tensor_tensor(out=v, in0=v, scalar=3.0, in1=ps[:, B_ST + n % 2, :],
                                            op0=ALU.add, op1=ALU.mult).then_inc(s["y_p"], 1)
                elif kind == "heads":
                    dve.wait_ge(s["o_tr"], at(b, 4, n + 1))
                    v = m.rearrange("p (a j r) -> p a j r", a=NT, r=32)
                    ve.reciprocal(orec[:, :, :], v[:, :, :, HD]).then_inc(s["o_rc"], 1)
                    dve.wait_ge(s["o_rc"], at(b, 4, n + 1))
                    ve.tensor_tensor(
                        a[:, :, n * HG * HD:(n + 1) * HG * HD].rearrange("p a (j d) -> p a j d", d=HD),
                        v[:, :, :, 0:HD], orec[:, :, :].unsqueeze(3).to_broadcast([P, NT, HG, HD]),
                        ALU.mult).then_inc(s["o_n"], 1)
                    if n == NG - 1:
                        wait(dve, s["xa2"], at(b, 1, 0))
                        ve.tensor_copy(mba[:, 0:M_VAL + 1], modb[:, bass.ds(index(b), 1), 0:M_VAL + 1].rearrange("p a b -> p (a b)"))\
                            .then_inc(s["mbar"], 1)
                elif kind == "add":
                    dve.wait_ge(s["proj"], at(b, 1, 1))
                    dve.wait_ge(s["mbar"], at(b, 1, 1))
                    dve.wait_ge(s["xa_in"], at(b, 16, 16))
                    wait(dve, s["x_out"], at(b, 16, 0))
                    g0 = l * M_PER + M_GA
                    ve.scalar_tensor_tensor(out=xe[:, :], in0=m, scalar=mba[:, g0:g0 + 1], in1=xa[:, :],
                                            op0=ALU.mult, op1=ALU.add).then_inc(s["xa1"], 1)
                    dve.wait_ge(s["xa1"], at(b, 1, 1))
                    ve.tensor_scalar(xe[:, :], xe[:, :], mba[:, g0 + 1:g0 + 2], None, ALU.add).then_inc(s["xa2"], 1)
                elif kind == "split":
                    w, c0, k = pieces(l)[n]
                    dve.wait_ge(wsp, split_count(l, n + 1))
                    part = whi[:, w, c0:c0 + k, :].rearrange("p a b -> p (a b)").bitcast(F32)
                    ve.tensor_tensor(wlo[:, w, c0:c0 + k, :].rearrange("p a b -> p (a b)"), staged(n), part,
                                     ALU.subtract).then_inc(wspd, 1)
                elif kind == "route1":
                    dve.wait_ge(s["rt_mm"], at(b, 1, 1))
                    lgp = m[:, 0:NT * E].rearrange("p (a b) -> p a b", a=NT)
                    if l == 0:
                        rt(s, l, b, 1, ve.tensor_copy(le, lgp))
                    else:
                        rt(s, l, b, 1, ve.tensor_tensor(le, lgp, rb[:, :].unsqueeze(1).to_broadcast([P, NT, E]),
                                                        ALU.add))
                    rt(s, l, b, 2, ve.tensor_reduce(r1[:, :], le, AX.X, ALU.max))
                    rt(s, l, b, RT_EXP, ve.tensor_tensor(le, le, bc(r1[:, :]), ALU.subtract))
                elif kind == "route2":
                    dve.wait_ge(s["rt_e"], at(b, 2 - l, 1))
                    rt(s, l, b, 4, ve.tensor_reduce(r1[:, :], ee, AX.X, ALU.add))
                    rt(s, l, b, 5, ve.reciprocal(r2[:, :], r1[:, :]))
                    rt(s, l, b, 6, ve.tensor_tensor(re, ee, bc(r2[:, :]), ALU.mult))
                elif kind == "route3":
                    dve.nop(nofuse=True)
                    for q in range(NT):
                        last = ve.max(top[:, q, :], rsc[:, q, 0:E])
                    rt(s, l, b, 7, last)
                    dve.nop(nofuse=True)
                    for q in range(NT):
                        last = ve.max_index(topi[:, q, :], top[:, q, :], rsc[:, q, 0:E])
                    rt(s, l, b, 8, last)
                    rt(s, l, b, 9, ve.tensor_copy(topf[:, :, :], topi[:, :, :]))
                elif kind == "route4":
                    iota = cst[:, C_IOTA:C_IOTA + E]
                    for q in range(NT):
                        last = ve.tensor_tensor(eq[:, q, 0:E, 0:K], iota.unsqueeze(2).to_broadcast([P, E, K]),
                                                topf[:, q, 0:K].unsqueeze(1).to_broadcast([P, E, K]), ALU.is_equal)
                    rt(s, l, b, 10, last)
                    rt(s, l, b, 11, ve.tensor_reduce(me, eq[:, :, 0:E, 0:K], AX.X, ALU.add))
                    if l == 0:
                        rt(s, l, b, RT_EXP2, ve.tensor_tensor(le, re, bc(top[:, :, 0]), ALU.subtract))
                    else:
                        rt(s, l, b, 12, ve.tensor_tensor(re, re, me, ALU.mult))
                elif kind == "route5":
                    if l == 0:
                        dve.wait_ge(s["rt_e"], at(b, 2, 2))
                        rt(s, l, b, 13, ve.tensor_tensor(re, ee, me, ALU.mult))
                    rt(s, l, b, 14 - l, ve.tensor_reduce(r1[:, :], re, AX.X, ALU.add))
                    if l == 1:
                        rt(s, l, b, 14, ve.tensor_scalar(r1[:, :], r1[:, :], 1e-12, None, ALU.max))
                    rt(s, l, b, RT_N[l], ve.reciprocal(r2[:, :], r1[:, :]))
                    ve.tensor_tensor(wd[:, :, 0:E], re, bc(r2[:, :]), ALU.mult).then_inc(s["w_c"], 1)
                elif kind == "silu":
                    dve.wait_ge(s["sil_r"], at(b, NCH, n + 1))
                    v = sil[:, n % 2, :]
                    ve.tensor_tensor(v, v, ps[:, B_G[l], :], ALU.mult).then_inc(s["a_r"], 1)
                elif kind == "hidden":
                    v = sil[:, n % 2, :]
                    if n < EC:
                        dve.wait_ge(s["t_r"], at(b, EC, n + 1))
                    else:
                        dve.wait_ge(s["a_r"], at(b, NCH, n + 1))
                    dve.wait_ge(s["u_mm"], at(b, NCH, n + 1))
                    if n >= 2:
                        dve.wait_ge(s["dn"], at(b, NCH, n - 1))
                    ve.tensor_tensor(hid[:, n % 2, :], v, ps[:, B_U[l], :], ALU.mult).then_inc(s["h_r"], 1)
                elif kind == "result":
                    dve.wait_ge(s["dn"], at(b, NCH, NCH))
                    g0 = l * M_PER + M_GB
                    ve.scalar_tensor_tensor(out=xe[:, :], in0=ps[:, B_ACC, :], scalar=mbx[:, g0:g0 + 1],
                                            in1=xe[:, :], op0=ALU.mult, op1=ALU.add).then_inc(s["xf"], 1)

            phases(dve, emit, lambda l, b: None)



RT_N = [15, 15]
RT_EXP = 3
RT_EXP2 = 12
PRE = {"hm": 24, "kd": 26, "qk": 27, "ax": 28, "psi": 29, "sq": 31, "lng": 33, "term": 36, "all": 39}


def layouts(np, d):
    z = {}
    x = d["L0_attn_x"]
    z["xT"] = x.transpose(0, 2, 1)

    def stack(w):
        s = np.zeros((P, NG, HG, 32), np.float32)
        v = w.reshape(P, NG, HG, HD)
        for r in range(3):
            s[:, :, :, COPY0 + HD * r:COPY0 + HD * (r + 1)] = v
        return s.reshape(P, 512)

    qkv = [d["L0_attn_Wqkv"], d["L1_attn_w_qkv"].T]
    wo = [d["L0_attn_Wproj"], d["L1_attn_w_out"].T]
    z["attw"] = np.stack([np.concatenate([stack(qkv[l][:, 0:P]), stack(qkv[l][:, P:2 * P]), qkv[l][:, 2 * P:], wo[l]],
                                         axis=1) for l in range(2)])
    z["alpha"] = np.repeat(d["L0_attn_alpha"].reshape(NG * HG, 1), 32, axis=1).reshape(512)
    z["beta"] = d["L0_attn_beta"]
    z["modw"] = np.stack([d["L0_wmod"], d["L1_wmod"]])
    c = np.zeros((P, C_COLS), np.float32)
    p = np.arange(P)
    c[:, C_ID:C_ID + P] = np.eye(P)
    c[:, C_ONES:C_ONES + P] = 1.0 / P
    row = p % 32
    c[:, C_LOQ] = (row >= COPY0 + 2 * HD)
    c[:, C_LOK] = (row >= COPY0 + HD) & (row < COPY0 + 2 * HD)
    c[:, C_LOS] = row == 1
    c[:, C_LOW] = (p >= 32) & (p < 64)
    c[:, C_ONE2] = row < SHIFT_ROWS
    c[:, C_ONE2 + 1] = EPS
    c[:, C_ONE2 + 2] = 1.0 / 3.0
    c[p, C_HEAD + p // HD] = 1.0
    c[p, C_RQ + p % HD] = 1.0
    c[p, C_RK + HD + p % HD] = 1.0
    for q in range(P):
        c[q % HD, C_RT + q] = 1.0
    for g in range(4):
        c[16 * g:16 * g + 16, C_BM + 16 * g:C_BM + 16 * g + 16] = 1.0 / 16
    c[:, C_IOTA:C_IOTA + 32] = np.arange(32)
    q = np.arange(64)
    c[q, C_SEL + q % 32] = 1.0
    z["consts"] = c
    k = np.zeros((P, K_COLS), np.float32)
    k[:, K_WQ:K_WQ + P] = qkv[0][:, 0:P]
    k[:, K_WK:K_WK + P] = qkv[0][:, P:2 * P]
    T = 4
    k[0:16, K_P1:K_P1 + 32] = d["L0_attn_Wphi1"].transpose(1, 0, 2).reshape(16, 32)
    k[0:16, K_A:K_A + 64] = d["L0_attn_A"].transpose(1, 0, 2).reshape(16, 64)
    for t in range(T):
        k[8 * t:8 * t + 8, K_P2 + 2 * t:K_P2 + 2 * t + 2] = d["L0_attn_Wphi2"][t]
        k[16 * t:16 * t + 16, K_PS1 + 16 * t:K_PS1 + 16 * t + 16] = d["L0_attn_Wpsi1"][t]
        k[16 * t:16 * t + 16, K_PS2 + 2 * t:K_PS2 + 2 * t + 2] = d["L0_attn_Wpsi2"][t]
    k[0:32, K_BP1] = d["L0_attn_bphi1"].reshape(32)
    k[0:8, K_BP2] = d["L0_attn_bphi2"].reshape(8)
    k[0:64, K_BS1] = d["L0_attn_bpsi1"].reshape(64)
    k[0:64, K_G] = d["L0_attn_ln_g"].reshape(64)
    k[0:64, K_B] = d["L0_attn_ln_b"].reshape(64)
    k[0:8, K_BS2] = d["L0_attn_bpsi2"].reshape(8)
    k[0:8, K_MIX] = np.repeat(d["L0_attn_mixing"], 2)
    k[0:8, K_TEMP] = d["L0_attn_temp_scale"]
    k[:, K_GAMMA] = np.repeat(d["L0_attn_gamma"], HD)
    k[:, K_BO] = d["L0_attn_bproj"]
    k[:, K_BO + 1] = d["L1_attn_b_out"]
    nb = x.shape[0]
    k[:, K_C:K_C + nb] = d["L0_c"].T
    k[:, K_C + nb:K_C + 2 * nb] = d["L1_c"].T
    z["kaw"] = k
    z["ffg"] = d["L0_ffn_kernel_gating_EDF"].transpose(1, 0, 2).reshape(P, -1)
    z["ffu"] = d["L0_ffn_kernel_up_EDF"].transpose(1, 0, 2).reshape(P, -1)
    z["ffd0"] = d["L0_ffn_kernel_down_EFD"].reshape(CHUNKS[0], P, P).transpose(1, 0, 2).reshape(P, -1)
    z["ffg1"] = np.concatenate([d["L1_ffn_gate_w"].transpose(2, 0, 1).reshape(P, -1), d["L1_ffn_sgate_w"].T], axis=1)
    z["ffu1"] = np.concatenate([d["L1_ffn_up_w"].transpose(2, 0, 1).reshape(P, -1), d["L1_ffn_sup_w"].T], axis=1)
    z["ffd1"] = np.concatenate([d["L1_ffn_down_w"].transpose(2, 0, 1).reshape(P, -1),
                                d["L1_ffn_sdown_w"].reshape(P, SHARED[1], P).transpose(2, 1, 0).reshape(P, -1)], axis=1)
    z["router0"] = d["L0_ffn_router_kernel_DE"]
    z["router1"] = d["L1_ffn_router_w"].T
    z["rbias"] = d["L1_ffn_router_bias"]
    return z


def kernel(**inputs):
    import numpy as _np
    import concourse.bacc as _bacc
    from concourse import mybir as _mybir
    from concourse.bass_utils import run_bass_kernel_spmd as _run

    nc = _bacc.Bacc("TRN2", target_bir_lowering=False, num_devices=1)
    z = layouts(_np, {k: _np.asarray(v) for k, v in inputs.items()})
    arrays, args = {}, {}
    for name, v in z.items():
        v = _np.ascontiguousarray(v)
        arrays[f"in_{name}"] = v
        args[name] = nc.dram_tensor(f"in_{name}", v.shape, _mybir.dt.from_np(v.dtype), kind="ExternalInput").ap()
    out = nc.dram_tensor("out_T", z["xT"].shape, _mybir.dt.float32, kind="ExternalOutput").ap()
    bass_adaln_two_layers_kernel(nc, outT=out, **args)
    r = _run(nc, [arrays], core_ids=[0])
    return r.results[0]["out_T"].transpose(0, 2, 1)
```
